# Optimizing a Trainium2 kernel written in Bass

```python
import numpy as np
import jax
import jax.numpy as jnp

def _softmax(x, axis=-1):
    return jax.nn.softmax(x, axis=axis)

def _gelu(x):
    return jax.nn.gelu(x, approximate=True)

def _silu(x):
    return jax.nn.silu(x)

def _sigmoid(x):
    return jax.nn.sigmoid(x)

def _layernorm(x, axis=-1, eps=1e-05):
    m = jnp.mean(x, axis=axis, keepdims=True)
    v = jnp.var(x, axis=axis, keepdims=True)
    return (x - m) / jnp.sqrt(v + eps)

def _scatter_add(tgt, idx, src, axis=0):
    return tgt.at[idx].add(src)

def _segment_sum(src, seg, n):
    return jax.ops.segment_sum(src, seg, n)
kernel_name = 'mk_gnn_preln_d2_gnn_r32_d6fd5d'

def setup_inputs(seed: int=0):
    np.random.seed(seed)
    _w = jnp.asarray

    def _rec_inputs():
        import jax
        import jax.numpy as jnp
        _gk = jax.random.key(seed)
        x = -0.0002928 + 1 * jax.random.normal(jax.random.fold_in(_gk, 1), (256, 512), jnp.float32)
        _s = jax.random.randint(jax.random.fold_in(_gk, 2), (2048,), 0, 256, jnp.int32)
        _d = jax.random.randint(jax.random.fold_in(_gk, 3), (2048,), 0, 256, jnp.int32)
        _loop = jnp.arange(256, dtype=jnp.int32)
        src = jnp.concatenate([_s, _d, _loop])
        dst = jnp.concatenate([_d, _s, _loop])
        _o = jnp.argsort(dst, stable=True)
        src = src[_o]
        dst = dst[_o]
        edge_attr_20 = 0.000389844 + 1.00025 * jax.random.normal(jax.random.fold_in(_gk, 12), (4352, 20), jnp.float32)
        edge_attr_4 = -0.00185629 + 0.998788 * jax.random.normal(jax.random.fold_in(_gk, 13), (4352, 4), jnp.float32)
        edge_weight = jax.random.uniform(jax.random.fold_in(_gk, 15), (4352,), jnp.float32, 0.0, 0.999993)
        return (x, src, dst, edge_attr_20, edge_attr_4, edge_weight)
    x, src, dst, edge_attr_20, edge_attr_4, edge_weight = _rec_inputs()

    def _L0_gnn_setup():
        import jax, jax.numpy as jnp
        import numpy as np
        N_NODES = 256
        N_EDGES = 8192
        D_IN = 512
        D_OUT = 512
        key = jax.random.key(seed)
        k1, k2, k3 = jax.random.split(key, 3)
        x = jax.random.normal(k1, (N_NODES, D_IN), dtype=jnp.float32)
        edge_index = jax.random.randint(k2, (2, N_EDGES), 0, N_NODES, dtype=jnp.int64)
        weight = jax.random.normal(k3, (D_IN, D_OUT), dtype=jnp.float32)
        bias = jnp.zeros((D_OUT,), dtype=jnp.float32)
        return {'x': x, 'edge_index': edge_index, 'weight': weight, 'bias': bias}
    _L0_gnn_all = _L0_gnn_setup()
    _L0_gnn_in = {k: v for k, v in _L0_gnn_all.items() if k in ('weight', 'bias')}
    del _L0_gnn_all

    def _L1_gnn_setup():
        import jax, jax.numpy as jnp
        import numpy as np
        import math
        B = 128
        F = 32
        R = 20
        N = 512
        E = 8192
        LOG2 = 0.6931471805599453
        IS2 = 1.0 / math.sqrt(2.0)
        IS3 = 1.0 / math.sqrt(3.0)
        IS6 = 1.0 / math.sqrt(6.0)

        def ssp(x):
            return jax.nn.softplus(x) - LOG2
        key = jax.random.key(seed)
        ks = jax.random.split(key, 14)
        return dict(x=jax.random.normal(ks[0], (N, 4 * B), jnp.float32), idx_i=jax.random.randint(ks[1], (E,), 0, N), idx_j=jax.random.randint(ks[2], (E,), 0, N), f_ij=jax.random.normal(ks[3], (E, R), jnp.float32), rcut_ij=jax.random.uniform(ks[4], (E,), jnp.float32), Yr_ij=jax.random.normal(ks[5], (E, 4), jnp.float32), w_in2f_s=jax.random.normal(ks[6], (B, F), jnp.float32), w_in2f_v=jax.random.normal(ks[7], (B, F), jnp.float32), W1=jax.random.normal(ks[8], (R, F), jnp.float32) / math.sqrt(R), b1=jnp.zeros((F,), jnp.float32), W2=jax.random.normal(ks[9], (F, 6 * F), jnp.float32) / math.sqrt(F), b2=jnp.zeros((6 * F,), jnp.float32), w_f2o1_s=jax.random.normal(ks[10], (2 * F, B), jnp.float32), w_f2o1_v=jax.random.normal(ks[11], (2 * F, B), jnp.float32), w_f2o2_s=jax.random.normal(ks[12], (B, B), jnp.float32), w_f2o2_v=jax.random.normal(ks[13], (B, B), jnp.float32))
    _L1_gnn_all = _L1_gnn_setup()
    _L1_gnn_in = {k: v for k, v in _L1_gnn_all.items() if k in ('w_in2f_s', 'w_in2f_v', 'W1', 'b1', 'W2', 'b2', 'w_f2o1_s', 'w_f2o1_v', 'w_f2o2_s', 'w_f2o2_v')}
    del _L1_gnn_all
    return {'x': x, 'src': src, 'dst': dst, 'edge_attr_20': edge_attr_20, 'edge_attr_4': edge_attr_4, 'edge_weight': edge_weight, 'L0_gnn_weight': _L0_gnn_in['weight'], 'L0_gnn_bias': _L0_gnn_in['bias'], 'L1_gnn_w_in2f_s': _L1_gnn_in['w_in2f_s'], 'L1_gnn_w_in2f_v': _L1_gnn_in['w_in2f_v'], 'L1_gnn_W1': _L1_gnn_in['W1'], 'L1_gnn_b1': _L1_gnn_in['b1'], 'L1_gnn_W2': _L1_gnn_in['W2'], 'L1_gnn_b2': _L1_gnn_in['b2'], 'L1_gnn_w_f2o1_s': _L1_gnn_in['w_f2o1_s'], 'L1_gnn_w_f2o1_v': _L1_gnn_in['w_f2o1_v'], 'L1_gnn_w_f2o2_s': _L1_gnn_in['w_f2o2_s'], 'L1_gnn_w_f2o2_v': _L1_gnn_in['w_f2o2_v']}

def reference(x, src, dst, edge_attr_20, edge_attr_4, edge_weight, L0_gnn_weight, L0_gnn_bias, L1_gnn_w_in2f_s, L1_gnn_w_in2f_v, L1_gnn_W1, L1_gnn_b1, L1_gnn_W2, L1_gnn_b2, L1_gnn_w_f2o1_s, L1_gnn_w_f2o1_v, L1_gnn_w_f2o2_s, L1_gnn_w_f2o2_v):
    import jax
    import jax.numpy as jnp

    def _L0_gnn_ref(x, edge_index, weight, bias):
        import jax, jax.numpy as jnp
        import numpy as np
        N_NODES = 256
        N_EDGES = 8192
        D_IN = 512
        D_OUT = 512
        n = x.shape[0]
        adj = jnp.zeros((n, n), dtype=x.dtype)
        adj = adj.at[edge_index[0], edge_index[1]].set(1.0)
        adj = adj.at[edge_index[1], edge_index[0]].set(1.0)
        adj = adj + jnp.eye(n, dtype=x.dtype)
        deg = jnp.sum(adj, axis=1)
        dinv = 1.0 / jnp.sqrt(deg)
        adj = adj * dinv[:, None] * dinv[None, :]
        return adj @ (x @ weight) + bias

    def _L1_gnn_ref(x, idx_i, idx_j, f_ij, rcut_ij, Yr_ij, w_in2f_s, w_in2f_v, W1, b1, W2, b2, w_f2o1_s, w_f2o1_v, w_f2o2_s, w_f2o2_v):
        import jax, jax.numpy as jnp
        import numpy as np
        import math
        B = 128
        F = 32
        R = 20
        N = 512
        E = 8192
        LOG2 = 0.6931471805599453
        IS2 = 1.0 / math.sqrt(2.0)
        IS3 = 1.0 / math.sqrt(3.0)
        IS6 = 1.0 / math.sqrt(6.0)

        def ssp(x):
            return jax.nn.softplus(x) - LOG2
        n = x.shape[0]
        xs = x[:, :B]
        xv = x[:, B:].reshape(n, B, 3)
        hs = xs @ w_in2f_s / math.sqrt(B)
        hv = jnp.einsum('nbc,bf->nfc', xv, w_in2f_v) / math.sqrt(B)
        s = hs[idx_j]
        v = hv[idx_j]
        ys = Yr_ij[:, 0]
        yv = Yr_ij[:, 1:4]
        t_s1 = s * ys[:, None]
        t_s2 = jnp.einsum('efc,ec->ef', v, yv) * IS3
        t_v1 = s[:, :, None] * yv[:, None, :]
        t_v2 = v * ys[:, None, None]
        t_pv = jnp.cross(v, yv[:, None, :]) * IS2
        ax, ay, az = (v[..., 0], v[..., 1], v[..., 2])
        bx, by, bz = (yv[:, None, 0:1], yv[:, None, 1:2], yv[:, None, 2:3])
        bx, by, bz = (bx[..., 0], by[..., 0], bz[..., 0])
        t_q = jnp.stack([(ax * by + ay * bx) * IS2, (ay * bz + az * by) * IS2, (2.0 * az * bz - ax * bx - ay * by) * IS6, (ax * bz + az * bx) * IS2, (ax * bx - ay * by) * IS2], axis=-1)
        h = ssp(f_ij @ W1 + b1)
        Wij = (h @ W2 + b2) * rcut_ij[:, None]
        Wf = Wij.reshape(-1, F, 6)
        edge = jnp.concatenate([(t_s1 * Wf[..., 0])[..., None], (t_s2 * Wf[..., 1])[..., None], t_v1 * Wf[..., 2:3], t_v2 * Wf[..., 3:4], t_pv * Wf[..., 4:5], t_q * Wf[..., 5:6]], axis=-1)
        agg = jax.ops.segment_sum(edge.reshape(edge.shape[0], -1), idx_i, num_segments=n).reshape(n, F, 16)
        s_in = jnp.concatenate([agg[..., 0], agg[..., 1]], axis=1)
        v_in = jnp.concatenate([agg[..., 2:5], agg[..., 5:8]], axis=1)
        os1 = s_in @ w_f2o1_s / math.sqrt(2 * F)
        ov1 = jnp.einsum('nmc,mb->nbc', v_in, w_f2o1_v) / math.sqrt(2 * F)
        os1 = ssp(os1)
        os2 = os1 @ w_f2o2_s / math.sqrt(B)
        ov2 = jnp.einsum('nbc,bd->ndc', ov1, w_f2o2_v) / math.sqrt(B)
        return jnp.concatenate([os2, ov2.reshape(n, -1)], axis=-1)
    edge_index = jnp.stack([src, dst])
    h = jnp.maximum(_layernorm(x, axis=-1), 0.0)
    x = x + _L0_gnn_ref(h, edge_index, L0_gnn_weight, L0_gnn_bias)
    h = jnp.maximum(_layernorm(x, axis=-1), 0.0)
    x = x + _L1_gnn_ref(h, src, dst, edge_attr_20, edge_weight, edge_attr_4, L1_gnn_w_in2f_s, L1_gnn_w_in2f_v, L1_gnn_W1, L1_gnn_b1, L1_gnn_W2, L1_gnn_b2, L1_gnn_w_f2o1_s, L1_gnn_w_f2o1_v, L1_gnn_w_f2o2_s, L1_gnn_w_f2o2_v)
    return x

_drawn_inputs = setup_inputs


def setup_inputs(seed=0):
    import zlib

    import numpy as np

    out = dict(_drawn_inputs(seed))
    spreads = {'L0_gnn_bias': (0.0, 0.75), 'L1_gnn_b1': (0.0, 0.8), 'L1_gnn_b2': (0.0, 0.464)}
    factors = {}
    for name, (base, spread) in spreads.items():
        noise = np.random.default_rng([zlib.crc32(name.encode()), seed]).standard_normal(out[name].shape)
        drawn = base * np.exp(spread * noise) if base else spread * noise
        out[name] = jnp.asarray(drawn.astype(out[name].dtype))
    for name, factor in factors.items():
        out[name] = (out[name] * factor).astype(out[name].dtype)
    return out
```

```python
import concourse.bass as bass
from concourse import mybir
from contextlib import ExitStack


def gnn_preln_kernel(nc, x, idx, dst_row, f_t, yr, rcut, w0, bias0, w1, w2, b2, w_in, w_o1s, w_o1vt, w_o2s, w_o2v,
                     ident, iota_row, iota_col, eye2, out):
    fp32 = mybir.dt.float32
    fp32r = mybir.dt.float32r
    bf16 = mybir.dt.bfloat16
    i32 = mybir.dt.int32
    ALU = mybir.AluOpType
    ACT = mybir.ActivationFunctionType

    P = 128
    N, D = x.shape
    NH = N // P
    KD = D // P
    T = idx.shape[1] // 2
    E = T * P
    TG = 4
    NG = (T + TG - 1) // TG
    F = w1.shape[1] // TG
    B = w_in.shape[0]
    C = 4 * F
    S = 8
    KF = f_t.shape[0]
    RG = 4
    LN_EPS = 1e-5
    IS3 = 3.0 ** -0.5
    SB = B ** -0.5
    SF = (2 * F) ** -0.5

    def tiles(g):
        return min(TG, T - TG * g)

    ctx = ExitStack()
    with ctx:
        def sb(name, shape, dt=fp32):
            return ctx.enter_context(nc.sbuf_tensor(name, shape, dt))

        def sem(name):
            return ctx.enter_context(nc.semaphore(name))

        x_sb = sb("x_sb", [P, NH, D])
        idx_sb = sb("idx_sb", [P, 2 * T], i32)
        dst_bc = sb("dst_bc", [P, E], i32)
        f_sb = sb("f_sb", [KF, NG * P])
        yr_sb = sb("yr_sb", [P, T, 4])
        rc_sb = sb("rc_sb", [P, T])
        w0_sb = sb("w0_sb", [P, KD, D])
        b0_sb = sb("b0_sb", [P, D])
        w1_sb = sb("w1_sb", [KF, P])
        w2_sb = sb("w2_sb", [P, TG * P])
        b2_sb = sb("b2_sb", [96, P])
        win_sb = sb("win_sb", [B, 2 * F])
        o1s_sb = sb("o1s_sb", [2 * F, B])
        o1vt_sb = sb("o1vt_sb", [B, P])
        o2s_sb = sb("o2s_sb", [B, B])
        o2v_sb = sb("o2v_sb", [B, B])
        id_sb = sb("id_sb", [P, P])
        iota_r = sb("iota_r", [P, N], bf16)
        iota_c = sb("iota_c", [P, NH])
        eye_sb = sb("eye_sb", [P, NH, N], bf16)
        idf = sb("idf", [P, 2 * T])
        idb = sb("idb", [P, P], bf16)
        dst_b = sb("dst_b", [P, E], bf16)
        Os = sb("Os", [P, T, N], bf16)
        onehot_dst = sb("onehot_dst", [P, T * N], bf16)
        Od = onehot_dst[:, :].rearrange("p (t n) -> p t n", t=T)
        OdT = onehot_dst[:, :].rearrange("p (a e) -> p a e", a=NH)
        OsR = sb("OsR", [P, RG, TG, N], fp32r)
        st6 = sb("st6", [P, NH, 6])
        mv1 = sb("mv1", [P, NH, 2])
        st6b = sb("st6b", [P, NH, 6])
        mv2 = sb("mv2", [P, NH, 2])
        h1 = sb("h1", [P, NH, D])
        h1T = sb("h1T", [P, NH, KD, P])
        xb = sb("xb", [P, NH, D])
        ve = sb("ve", [P, NH])
        rstd1 = sb("rstd1", [P, NH])
        neghalf = sb("neghalf", [P, NH])
        CI = sb("CI", [P, NH, N], bf16)
        A = sb("A", [P, NH, N], fp32r)
        deg = sb("deg", [P, NH])
        dinv = sb("dinv", [P, NH])
        s1 = sb("s1", [P, NH])
        hW_hi = sb("hW_hi", [P, NH, D], fp32r)
        hW_lo = sb("hW_lo", [P, NH, D], fp32r)
        x1 = sb("x1", [P, NH, D])
        xsum = sb("xsum", [P, NH])
        mean2 = sb("mean2", [P, NH])
        h2, h2T = h1, h1T
        ve2 = sb("ve2", [P, NH])
        s2 = sb("s2", [P, NH])
        s2p = sb("s2p", [P, NH])
        Hf = sb("Hf", [P, NH, C])
        Hr = sb("Hr", [P, NH, C])
        Hp = [sb(f"Hp{i}", [P, NH, C], bf16) for i in range(3)]
        za = sb("za", [P, NG * P])
        hT = sb("hT", [P, NG * P])
        ones = sb("ones", [96, P], bf16)
        b2h = sb("b2h", [96, P], bf16)
        b2m = sb("b2m", [96, P], bf16)
        b2r = sb("b2r", [96, P])
        b2p = sb("b2p", [96, P], bf16)
        y = sb("y", [P, T, 4])
        Wsb = sb("Wsb", [P, RG, TG * P])
        WY = sb("WY", [P, T, S * F])
        late = dst_bc[:].bitcast(fp32)
        M = late[:, 0:2 * TG * S * F].rearrange("p (o t n) -> p o t n", o=2, t=TG)
        tmp = late[:, 2 * TG * S * F:2 * TG * (S + 3) * F].rearrange("p (o t n) -> p o t n", o=2, t=TG)
        Mh = sb("Mh", [P, 2, TG, S * F], fp32r)
        Ml = sb("Ml", [P, 2, TG, S * F], fp32r)
        aggT = sb("aggT", [P, 2, N])
        wc_sb = sb("wc_sb", [P, B])
        ta, te, te2, os1T = (za[:, i * N:(i + 1) * N] for i in range(4))
        o_sb = x_sb
        warm = sb("warm", [P, 1])

        bank = [ctx.enter_context(nc.psum_tensor(f"bank{i}", [P, 512], fp32)) for i in range(8)]
        bT = bank[6][:, :].bitcast(bf16)

        (d_x, d_idx, d_dst, d_f, d_yr, d_w0, d_b0, d_w1, d_w2, d_b2, d_win, d_o1s, d_o1v, d_o2s, d_o2v, d_id,
         d_ir, d_ic, d_eye, d_rc, d_out) = [sem("dma_" + n) for n in
                                            "x idx dst f yr w0 b0 w1 w2 b2 win o1s o1v o2s o2v id ir ic eye rc out".split()]
        names = ("idf idb st mv1 h1 tp1 h1T hW onehot adj CI CT A ve rstd dinv s1 hWr hW_hi hW_lo L0 xb x1 mean2 h2 tp2 h2T "
                 "st2 mv2 ve2 s2p s2 H Hf Hp0 Hr Hp1 Hp2 z zabs zexp zln hT ones b2h b2r b2m b2r2 b2p b2q W Wsb y WY dstb OdT OsR "
                 "G prod M Mh Ml scat aggT wc wcs os1 ta te tl os1T fin os2 o o1 nh warm y1")
        q = {n: sem("s_" + n) for n in names.split()}

        block = ctx.enter_context(nc.Block())

        @block.sync
        def _(sp):
            sp.dma_start(f_sb[:], f_t).then_inc(d_f, 16)
            sp.dma_start(idx_sb[:], idx).then_inc(d_idx, 16)
            sp.dma_start(x_sb[:, :, :], x.rearrange("(a p) d -> p a d", p=P)).then_inc(d_x, 16)
            sp.dma_start(w0_sb[:, :, :], w0.rearrange("(k p) n -> p k n", p=P)).then_inc(d_w0, 16)
            sp.dma_start(dst_bc[:], dst_row.broadcast_to((P, E))).then_inc(d_dst, 16)
            sp.dma_start(b0_sb[:], bias0.broadcast_to((P, D))).then_inc(d_b0, 16)
            sp.dma_start(win_sb[:], w_in).then_inc(d_win, 16)
            sp.dma_start(o1s_sb[:], w_o1s).then_inc(d_o1s, 16)
            sp.dma_start(o1vt_sb[:], w_o1vt).then_inc(d_o1v, 16)
            sp.dma_start(o2s_sb[:], w_o2s).then_inc(d_o2s, 16)
            sp.dma_start(o2v_sb[:], w_o2v).then_inc(d_o2v, 16)
            for a in range(NH):
                sp.wait_ge(q["o"], a + 1)
                sp.dma_start(out[a * P:(a + 1) * P, :], o_sb[:, a, :]).then_inc(d_out, 16)
            sp.wait_ge(d_out, 16 * NH)

        @block.scalar
        def _(act):
            act.dma_start(w1_sb[:], w1).then_inc(d_w1, 16)
            act.dma_start(iota_r[:], iota_row).then_inc(d_ir, 16)
            act.dma_start(id_sb[:], ident).then_inc(d_id, 16)
            act.dma_start(w2_sb[:], w2).then_inc(d_w2, 16)
            act.dma_start(b2_sb[:], b2).then_inc(d_b2, 16)
            act.dma_start(yr_sb[:, :, :], yr).then_inc(d_yr, 16)
            act.dma_start(rc_sb[:], rcut).then_inc(d_rc, 16)
            act.dma_start(eye_sb[:, :, :], eye2).then_inc(d_eye, 16)
            act.dma_start(iota_c[:], iota_col).then_inc(d_ic, 16)
            for c in range(3):
                lo, hi = 512 * c, min(512 * (c + 1), NG * P)
                act.wait_ge(q["z"], c + 1)
                nc.scalar.activation(za[:, lo:hi], bank[2 + c][:, 0:hi - lo], ACT.Abs).then_inc(q["zabs"], 1)
            act.wait_ge(q["zabs"], 3)
            nc.scalar.activation(za[:], za[:], ACT.Exp, scale=-1.0).then_inc(q["zexp"], 1)
            act.wait_ge(q["zexp"], 1)
            act.wait_ge(q["nh"], 1)
            nc.scalar.activation(za[:], za[:], ACT.Ln, bias=warm[:, 0:1], scale=0.5).then_inc(q["zln"], 1)
            for a in range(NH):
                act.wait_ge(q["tp1"], a + 1)
                nc.scalar.activation(h1T[:, a, :, :], bank[6 + a][:, :], ACT.Copy).then_inc(q["h1T"], 1)
            for g in range(NG):
                t0, n = TG * g, tiles(g)
                act.wait_ge(q["W"], g + 1)
                if g >= RG:
                    act.wait_ge(q["WY"], g - RG + 1)
                nc.scalar.activation(Wsb[:, g % RG, 0:n * P], bank[2 + g % 2][:, 0:n * P], ACT.Copy).then_inc(q["Wsb"], 1)
                if g == 2:
                    act.wait_ge(d_dst, 16)
                    nc.scalar.activation(dst_b[:], dst_bc[:], ACT.Copy).then_inc(q["dstb"], 1)
            def scatter_onehots(g):
                t0, n = TG * g, tiles(g)
                act.wait_ge(q["onehot"], 2 * (t0 + n))
                if g >= RG:
                    act.wait_ge(q["scat"], g - RG + 1)
                nc.scalar.activation(OsR[:, g % RG, 0:n, :], Os[:, t0:t0 + n, :], ACT.Copy).then_inc(q["OsR"], 1)

            for g in range(RG):
                scatter_onehots(g)
            for a in range(NH):
                act.wait_ge(q["s1"], 1)
                nc.scalar.activation(hW_hi[:, a, :], bank[a][:, :], ACT.Copy, scale=s1[:, a:a + 1]).then_inc(q["hW_hi"], 1)
            act.wait_ge(q["tp2"], 1)
            nc.scalar.activation(h2T[:, 0, :, :], bank[6][:, :], ACT.Copy).then_inc(q["h2T"], 1)
            act.wait_ge(q["wc"], 1)
            nc.scalar.activation(wc_sb[:], bank[3][:, 0:B], ACT.Copy, scale=SF * SB).then_inc(q["wcs"], 1)
            for g in range(NG):
                n = tiles(g)
                act.wait_ge(q["M"], g + 1)
                if g >= 2:
                    act.wait_ge(q["scat"], g - 1)
                nc.scalar.activation(Mh[:, g % 2, 0:n, :], M[:, g % 2, 0:n, :], ACT.Copy).then_inc(q["Mh"], 1)
                if 1 <= g and g + RG - 1 < NG:
                    scatter_onehots(g + RG - 1)
            act.wait_ge(q["scat"], NG)
            nc.scalar.activation(aggT[:, 1, :], bank[5][:, 0:N], ACT.Copy).then_inc(q["aggT"], 1)
            act.wait_ge(q["os1"], 1)
            nc.scalar.activation(ta[:], bank[2][:, 0:N], ACT.Abs, scale=SF).then_inc(q["ta"], 1)
            act.wait_ge(q["ta"], 1)
            nc.scalar.activation(te[:], ta[:], ACT.Exp, scale=-1.0).then_inc(q["te"], 1)
            act.wait_ge(q["te"], 1)
            nc.scalar.activation(ta[:], te[:], ACT.Ln, bias=warm[:, 0:1], scale=0.5).then_inc(q["tl"], 1)

        @block.gpsimd
        def _(pool):
            nc.gpsimd.memset(warm[:], 0.5).then_inc(q["nh"], 1)
            nc.gpsimd.memset(neghalf[:], -0.5).then_inc(q["nh"], 1)
            nc.gpsimd.memset(ones[:], 1.0).then_inc(q["ones"], 1)
            pool.wait_ge(d_b2, 16)
            nc.gpsimd.tensor_copy(b2h[:], b2_sb[:]).then_inc(q["b2h"], 1)
            pool.wait_ge(q["b2h"], 1)
            nc.gpsimd.tensor_tensor(b2r[:], b2_sb[:], b2h[:], ALU.subtract).then_inc(q["b2r"], 1)
            pool.wait_ge(q["b2r"], 1)
            nc.gpsimd.tensor_copy(b2m[:], b2r[:]).then_inc(q["b2m"], 1)
            pool.wait_ge(q["b2m"], 1)
            nc.gpsimd.tensor_copy(b2p[0:32, :], b2h[0:32, :]).then_inc(q["b2p"], 1)
            pool.wait_ge(q["b2p"], 1)
            nc.gpsimd.tensor_copy(b2p[32:64, :], b2m[32:64, :]).then_inc(q["b2p"], 1)
            pool.wait_ge(q["b2p"], 2)
            nc.gpsimd.tensor_tensor(b2p[64:96, :], b2r[64:96, :], b2m[64:96, :], ALU.subtract).then_inc(q["b2p"], 1)
            pool.wait_ge(q["b2p"], 3)
            pool.wait_ge(d_yr, 16)
            pool.wait_ge(d_rc, 16)
            nc.gpsimd.tensor_tensor(y[:, :, :], yr_sb[:, :, :], rc_sb[:].unsqueeze(2).broadcast_to((P, T, 4)),
                                    ALU.mult).then_inc(q["y"], 1)
            pool.wait_ge(q["mv1"], NH)
            pool.wait_ge(q["nh"], 2)
            nc.gpsimd.tensor_scalar(ve[:], mv1[:, :, 1], LN_EPS, None, ALU.add).then_inc(q["ve"], 1)
            pool.wait_ge(q["ve"], 1)
            nc.gpsimd.tensor_tensor(rstd1[:], ve[:], neghalf[:], ALU.pow).then_inc(q["rstd"], 1)
            pool.wait_ge(d_b0, 16)
            nc.gpsimd.tensor_tensor(xb[:, :, :], x_sb[:, :, :], b0_sb[:].unsqueeze(1).broadcast_to((P, NH, D)),
                                    ALU.add).then_inc(q["xb"], 1)

            def filters(g):
                t0, n = TG * g, tiles(g)
                pool.wait_ge(q["Wsb"], g + 1)
                if g == 0:
                    pool.wait_ge(q["y"], 1)
                w = Wsb[:, g % RG, 0:n * P].rearrange("p (t k f) -> p t k f", t=n, k=4)
                wy = WY[:, t0:t0 + n, :].rearrange("p t (k f) -> p t k f", k=S)
                yv = y[:, t0:t0 + n, 1:4].unsqueeze(3).broadcast_to((P, n, 3, F))
                y0 = y[:, t0:t0 + n, 0:1].unsqueeze(3).broadcast_to((P, n, 2, F))
                nc.gpsimd.tensor_tensor(wy[:, :, 0:8:4, :], w[:, :, 0:2, :], y0, ALU.mult)
                nc.gpsimd.tensor_tensor(wy[:, :, 1:4, :], w[:, :, 2:3, :].broadcast_to((P, n, 3, F)), yv, ALU.mult)
                nc.gpsimd.tensor_tensor(wy[:, :, 5:8, :], w[:, :, 3:4, :].broadcast_to((P, n, 3, F)), yv,
                                        ALU.mult).then_inc(q["WY"], 1)

            for g in range(NG):
                filters(g)
                if g == 6:
                    pool.wait_ge(q["A"], NH)
                    nc.gpsimd.tensor_tensor(dinv[:], deg[:], neghalf[:], ALU.pow).then_inc(q["dinv"], 1)
                    pool.wait_ge(q["dinv"], 1)
                    pool.wait_ge(q["rstd"], 1)
                    nc.gpsimd.tensor_tensor(s1[:], dinv[:], rstd1[:], ALU.mult).then_inc(q["s1"], 1)
            pool.wait_ge(q["mv2"], NH)
            nc.gpsimd.tensor_scalar(ve2[:], mv2[:, :, 1], LN_EPS, None, ALU.add).then_inc(q["ve2"], 1)
            pool.wait_ge(q["ve2"], 1)
            nc.gpsimd.tensor_tensor(s2p[:], ve2[:], neghalf[:], ALU.pow).then_inc(q["s2p"], 1)
            pool.wait_ge(q["s2p"], 1)
            nc.gpsimd.tensor_scalar(s2[:], s2p[:], SB, None, ALU.mult).then_inc(q["s2"], 1)
            for g in range(NG):
                n = tiles(g)
                pool.wait_ge(q["Mh"], g + 1)
                if g >= 2:
                    pool.wait_ge(q["scat"], g - 1)
                nc.gpsimd.tensor_tensor(Ml[:, g % 2, 0:n, :], M[:, g % 2, 0:n, :], Mh[:, g % 2, 0:n, :].bitcast(fp32),
                                        ALU.subtract).then_inc(q["Ml"], 1)

        @block.vector
        def _(dve):
            dve.wait_ge(d_idx, 16)
            nc.vector.tensor_copy(idf[:], idx_sb[:]).then_inc(q["idf"], 1)
            dve.wait_ge(d_id, 16)
            nc.vector.tensor_copy(idb[:], id_sb[:]).then_inc(q["idb"], 1)
            dve.wait_ge(d_x, 16)
            for a in range(NH):
                nc.vector.bn_stats(st6[:, a, :], x_sb[:, a, :]).then_inc(q["st"], 1)
            for a in range(NH):
                dve.wait_ge(q["st"], a + 1)
                nc.vector.bn_aggr(mv1[:, a, :], st6[:, a, :]).then_inc(q["mv1"], 1)
            for a in range(NH):
                dve.wait_ge(q["mv1"], a + 1)
                nc.vector.tensor_scalar(h1[:, a, :], x_sb[:, a, :], mv1[:, a, 0:1], 0.0, ALU.subtract,
                                        ALU.max).then_inc(q["h1"], 1)
            dve.wait_ge(q["idf"], 1)
            dve.wait_ge(d_ir, 16)
            for t in range(T):
                nc.vector.tensor_scalar(Os[:, t, :], iota_r[:], idf[:, t:t + 1], None, ALU.is_equal).then_inc(q["onehot"], 1)
                nc.vector.tensor_scalar(Od[:, t, :], iota_r[:], idf[:, T + t:T + t + 1], None,
                                        ALU.is_equal).then_inc(q["onehot"], 1)
                if t == 12:
                    dve.wait_ge(q["zln"], 1)
                    for c in range(3):
                        lo, hi = 512 * c, min(512 * (c + 1), NG * P)
                        nc.vector.scalar_tensor_tensor(hT[:, lo:hi], bank[2 + c][:, 0:hi - lo], 0.0, za[:, lo:hi],
                                                       ALU.max, ALU.add).then_inc(q["hT"], 1)
            dve.wait_ge(d_o1s, 16)
            nc.vector.tensor_scalar(o1s_sb[F:2 * F, :], o1s_sb[F:2 * F, :], IS3, None, ALU.mult).then_inc(q["o1"], 1)
            dve.wait_ge(d_eye, 16)
            dve.wait_ge(q["adj"], 1)
            for a in range(NH):
                nc.vector.scalar_tensor_tensor(CI[:, a, :], bank[4 + a][:, 0:N], 1.0, eye_sb[:, a, :], ALU.min,
                                               ALU.add).then_inc(q["CI"], 1)
            dve.wait_ge(d_ic, 16)
            dve.wait_ge(q["dstb"], 1)
            nc.vector.tensor_scalar(OdT[:, 0, :], dst_b[:], iota_c[:, 0:1], None, ALU.is_equal).then_inc(q["OdT"], 1)
            dve.wait_ge(q["CT"], 1)
            for a in range(NH):
                dve.wait_ge(q["CI"], a + 1)
                nc.vector.scalar_tensor_tensor(A[:, a, :], bT[:, a * N:(a + 1) * N], 0.0, CI[:, a, :], ALU.add,
                                               ALU.max, accum_out=deg[:, a:a + 1]).then_inc(q["A"], 1)
            nc.vector.tensor_scalar(OdT[:, 1, :], dst_b[:], iota_c[:, 1:2], None, ALU.is_equal).then_inc(q["OdT"], 1)
            dve.wait_ge(q["s1"], 1)
            for a in range(NH):
                dve.wait_ge(q["hW_hi"], a + 1)
                nc.vector.scalar_tensor_tensor(hW_lo[:, a, :], bank[a][:, :], s1[:, a:a + 1],
                                               hW_hi[:, a, :].bitcast(fp32), ALU.mult, ALU.subtract).then_inc(q["hW_lo"], 1)
            dve.wait_ge(q["xb"], 1)
            for a in range(NH):
                dve.wait_ge(q["L0"], a + 1)
                nc.vector.scalar_tensor_tensor(x1[:, a, :], bank[a][:, :], dinv[:, a:a + 1], xb[:, a, :], ALU.mult,
                                               ALU.add, accum_out=xsum[:, a:a + 1]).then_inc(q["x1"], 1)
                dve.wait_ge(q["x1"], a + 1)
                nc.vector.tensor_scalar(mean2[:, a:a + 1], xsum[:, a:a + 1], 1.0 / D, None, ALU.mult).then_inc(q["mean2"], 1)
                dve.wait_ge(q["mean2"], a + 1)
                nc.vector.tensor_scalar(h2[:, a, :], x1[:, a, :], mean2[:, a:a + 1], 0.0, ALU.subtract,
                                        ALU.max).then_inc(q["h2"], 1)
            for a in range(NH):
                nc.vector.bn_stats(st6b[:, a, :], x1[:, a, :]).then_inc(q["st2"], 1)
            for a in range(NH):
                dve.wait_ge(q["st2"], a + 1)
                nc.vector.bn_aggr(mv2[:, a, :], st6b[:, a, :]).then_inc(q["mv2"], 1)
            dve.wait_ge(q["tp2"], 2)
            nc.vector.tensor_copy(h2T[:, 1, :, :], bank[7][:, :]).then_inc(q["h2T"], 1)
            dve.wait_ge(q["s2"], 1)
            dve.wait_ge(q["H"], 1)
            for a in range(NH):
                nc.vector.tensor_scalar(Hf[:, a, :], bank[2][:, a * C:(a + 1) * C], s2[:, a:a + 1], None,
                                        ALU.mult).then_inc(q["Hf"], 1)
            dve.wait_ge(q["Hf"], NH)
            nc.vector.tensor_copy(Hp[0][:, :, :], Hf[:, :, :]).then_inc(q["Hp0"], 1)
            dve.wait_ge(q["Hp0"], 1)
            nc.vector.tensor_tensor(Hr[:, :, :], Hf[:, :, :], Hp[0][:, :, :], ALU.subtract).then_inc(q["Hr"], 1)
            dve.wait_ge(q["Hr"], 1)
            nc.vector.tensor_copy(Hp[1][:, :, :], Hr[:, :, :]).then_inc(q["Hp1"], 1)
            dve.wait_ge(q["Hp1"], 1)
            nc.vector.tensor_tensor(Hp[2][:, :, :], Hr[:, :, :], Hp[1][:, :, :], ALU.subtract).then_inc(q["Hp2"], 1)
            for g in range(NG):
                t0, n, o = TG * g, tiles(g), g % 2
                G = bank[o][:, 0:n * C].rearrange("p (t c f) -> p t c f", t=n, c=4)
                wy = WY[:, t0:t0 + n, :].rearrange("p t (k f) -> p t k f", k=S)
                m = M[:, o, 0:n, :].rearrange("p t (k f) -> p t k f", k=S)
                tc = tmp[:, o, 0:n, :].rearrange("p t (c f) -> p t c f", c=3)
                dve.wait_ge(q["G"], g + 1)
                dve.wait_ge(q["WY"], g + 1)
                if g >= 2:
                    dve.wait_ge(q["Ml"], g - 1)
                nc.vector.tensor_tensor(tc, G[:, :, 1:4, :], wy[:, :, 5:8, :], ALU.mult).then_inc(q["y1"], 1)
                nc.vector.tensor_tensor(m[:, :, 0:8:2, :], G[:, :, 0:1, :].broadcast_to((P, n, 4, F)), wy[:, :, 0:4, :],
                                        ALU.mult)
                nc.vector.tensor_tensor(m[:, :, 3:8:2, :], G[:, :, 1:4, :], wy[:, :, 4:5, :].broadcast_to((P, n, 3, F)),
                                        ALU.mult).then_inc(q["prod"], 1)
                dve.wait_ge(q["y1"], g + 1)
                nc.vector.tensor_reduce(m[:, :, 1, :], tc.rearrange("p t c f -> p t f c"), mybir.AxisListType.X,
                                        ALU.add).then_inc(q["M"], 1)
            dve.wait_ge(q["scat"], NG)
            nc.vector.tensor_copy(aggT[:, 0, :], bank[4][:, 0:N]).then_inc(q["aggT"], 1)
            dve.wait_ge(q["ta"], 1)
            nc.vector.tensor_scalar(te2[:], bank[2][:, 0:N], SF, 0.0, ALU.mult, ALU.max).then_inc(q["b2q"], 1)
            dve.wait_ge(q["tl"], 1)
            dve.wait_ge(q["b2q"], 1)
            nc.vector.tensor_tensor(os1T[:], te2[:], ta[:], ALU.add).then_inc(q["os1T"], 1)
            for a in range(NH):
                dve.wait_ge(q["fin"], a + 1)
                ov = o_sb[:, a, B:].rearrange("p (d c) -> p c d", c=3)
                xv = x1[:, a, B:].rearrange("p (d c) -> p c d", c=3)
                xz = bank[a][:, 0:2 * B].rearrange("p (c d) -> p c d", c=2)
                nc.vector.tensor_tensor(ov[:, 0:3:2, :], xz, xv[:, 0:3:2, :], ALU.add)
                nc.vector.tensor_tensor(ov[:, 1, :], bank[6 + a][:, 0:B], xv[:, 1, :], ALU.add)
            for a in range(NH):
                dve.wait_ge(q["os2"], a + 1)
                nc.vector.scalar_tensor_tensor(o_sb[:, a, 0:B], bank[2 + a][:, 0:B], SB, x1[:, a, 0:B], ALU.mult,
                                               ALU.add).then_inc(q["o"], 1)

        @block.tensor
        def _(pe):
            pe.wait_ge(d_f, 16)
            pe.wait_ge(d_w1, 16)
            for c in range(3):
                lo, hi = 512 * c, min(512 * (c + 1), NG * P)
                nc.tensor.matmul(bank[2 + c][:, 0:hi - lo], w1_sb[:], f_sb[:, lo:hi], start=True, stop=True).then_inc(q["z"], 1)
            pe.wait_ge(d_id, 16)
            for a in range(NH):
                pe.wait_ge(q["h1"], a + 1)
                for k in range(KD):
                    last = nc.tensor.transpose(bank[6 + a][:, k * P:(k + 1) * P], h1[:, a, k * P:(k + 1) * P], id_sb[:])
                last.then_inc(q["tp1"], 1)
            pe.wait_ge(d_w0, 16)
            for a in range(NH):
                pe.wait_ge(q["h1T"], a + 1)
                for k in range(KD):
                    last = nc.tensor.matmul(bank[a][:, :], h1T[:, a, k, :], w0_sb[:, k, :], start=(k == 0), stop=(k == KD - 1))
                last.then_inc(q["hW"], 1)

            def adjacency(t0, t1):
                for t in range(t0, t1):
                    pe.wait_ge(q["onehot"], 2 * t + 2)
                    for a in range(NH):
                        last = nc.tensor.matmul(bank[4 + a][:, 0:N], Os[:, t, a * P:(a + 1) * P], Od[:, t, :],
                                                start=(t == 0), stop=(t == T - 1))
                if t1 == T:
                    last.then_inc(q["adj"], 1)

            def filters(g):
                n = tiles(g)
                k = 32 * n
                if g == 0:
                    pe.wait_ge(q["hT"], 3)
                    pe.wait_ge(d_w2, 16)
                    pe.wait_ge(q["b2p"], 3)
                if g >= 2:
                    pe.wait_ge(q["Wsb"], g - 1)
                ps = bank[2 + g % 2][:, 0:n * P]
                nc.tensor.matmul(ps, ones[:], b2p[:].unsqueeze(1).broadcast_to((96, n, P)), start=True, stop=False)
                nc.tensor.matmul(ps, hT[0:k, g * P:(g + 1) * P], w2_sb[0:k, 0:n * P], start=False, stop=True).then_inc(q["W"], 1)

            pe.wait_ge(q["hT"], 3)
            for g in range(NG):
                filters(g)
                adjacency(4 * g if g < 8 else 32, 4 * g + 4 if g < 8 else T)
            pe.wait_ge(q["idb"], 1)
            pe.wait_ge(q["CI"], NH)
            for a in range(NH):
                for b in range(NH):
                    last = nc.tensor.transpose(bT[:, a * N + b * P:a * N + (b + 1) * P], CI[:, b, a * P:(a + 1) * P], idb[:])
            last.then_inc(q["CT"], 1)
            pe.wait_ge(q["A"], NH)
            pe.wait_ge(q["hW_hi"], NH)
            pe.wait_ge(q["hW_lo"], NH)
            for a in range(NH):
                for b in range(NH):
                    for part in (hW_hi, hW_lo):
                        last = nc.tensor.matmul(bank[a][:, :], A[:, b, a * P:(a + 1) * P], part[:, b, :],
                                                start=(b == 0 and part is hW_hi), stop=(b == NH - 1 and part is hW_lo))
                last.then_inc(q["L0"], 1)
            pe.wait_ge(d_o1v, 16)
            pe.wait_ge(d_o2v, 16)
            pe.wait_ge(q["Wsb"], NG)
            nc.tensor.matmul(bank[3][:, 0:B], o1vt_sb[:], o2v_sb[:], start=True, stop=True).then_inc(q["wc"], 1)
            for a in range(NH):
                pe.wait_ge(q["h2"], a + 1)
                for k in range(4):
                    src = h2[:, a, 0:B] if k == 0 else h2[:, a, B:].rearrange("p (b c) -> p c b", c=3)[:, k - 1, :]
                    last = nc.tensor.transpose(bank[6 + a][:, k * P:(k + 1) * P], src, id_sb[:])
                last.then_inc(q["tp2"], 1)
            pe.wait_ge(d_win, 16)
            pe.wait_ge(q["h2T"], NH)
            for a in range(NH):
                for k in range(4):
                    w = win_sb[:, 0:F] if k == 0 else win_sb[:, F:2 * F]
                    last = nc.tensor.matmul(bank[2][:, a * C + k * F:a * C + (k + 1) * F], h2T[:, a, k, :], w,
                                            start=True, stop=True)
            last.then_inc(q["H"], 1)

            def gather(g):
                pe.wait_ge(q["OdT"], NH)
                pe.wait_ge(q["Hp2"], 1)
                if g >= 2:
                    pe.wait_ge(q["prod"], g - 1)
                for j in range(tiles(g)):
                    t = TG * g + j
                    for a in range(NH):
                        for i in range(3):
                            last = nc.tensor.matmul(bank[g % 2][:, j * C:(j + 1) * C], OdT[:, a, t * P:(t + 1) * P],
                                                    Hp[i][:, a, :], start=(a == 0 and i == 0), stop=(a == NH - 1 and i == 2))
                last.then_inc(q["G"], 1)

            def scatter(g):
                pe.wait_ge(q["Mh"], g + 1)
                pe.wait_ge(q["Ml"], g + 1)
                pe.wait_ge(q["OsR"], g + 1)
                for j in range(tiles(g)):
                    t = TG * g + j
                    for b in range(2):
                        for part in (Mh, Ml):
                            last = nc.tensor.matmul(bank[4 + b][:, 0:N], part[:, g % 2, j, b * P:(b + 1) * P], OsR[:, g % RG, j, :],
                                                    start=(t == 0 and part is Mh), stop=(t == T - 1 and part is Ml))
                last.then_inc(q["scat"], 1)

            gather(0)
            for g in range(1, NG):
                gather(g)
                scatter(g - 1)
            scatter(NG - 1)
            pe.wait_ge(q["aggT"], 2)
            pe.wait_ge(q["o1"], 1)
            nc.tensor.matmul(bank[2][:, 0:N], o1s_sb[:], aggT[0:64, 0, :], start=True, stop=True).then_inc(q["os1"], 1)
            pe.wait_ge(q["wcs"], 1)
            pe.wait_ge(d_o2s, 16)
            for a in range(NH):
                n = slice(a * P, (a + 1) * P)
                nc.tensor.matmul(bank[a][:, 0:B], aggT[64:128, 0, n], wc_sb[64:128, :], start=True, stop=True)
                nc.tensor.matmul(bank[a][:, B:2 * B], aggT[64:128, 1, n], wc_sb[64:128, :], start=True, stop=True)
                nc.tensor.matmul(bank[6 + a][:, 0:B], aggT[0:64, 1, n], wc_sb[0:64, :], start=True,
                                 stop=True).then_inc(q["fin"], 1)
            pe.wait_ge(q["os1T"], 1)
            for a in range(NH):
                n = slice(a * P, (a + 1) * P)
                nc.tensor.matmul(bank[2 + a][:, 0:B], os1T[:, n], o2s_sb[:], start=True, stop=True).then_inc(q["os2"], 1)


def kernel(x, src, dst, edge_attr_20, edge_attr_4, edge_weight, L0_gnn_weight, L0_gnn_bias, L1_gnn_w_in2f_s,
           L1_gnn_w_in2f_v, L1_gnn_W1, L1_gnn_b1, L1_gnn_W2, L1_gnn_b2, L1_gnn_w_f2o1_s, L1_gnn_w_f2o1_v,
           L1_gnn_w_f2o2_s, L1_gnn_w_f2o2_v):
    import ml_dtypes
    import numpy as np
    import concourse.bacc as bacc
    from concourse.bass_utils import run_bass_kernel_spmd

    g = {k: np.asarray(v) for k, v in locals().items() if isinstance(v, object) and hasattr(v, "shape")}
    P, TG = 128, 4
    E, R = g["edge_attr_20"].shape
    F = g["L1_gnn_W1"].shape[1]
    T = E // P
    NG = -(-T // TG)
    N = g["x"].shape[0]

    def edges_on_partitions(a):
        return np.ascontiguousarray(np.moveaxis(a.reshape(T, P, *a.shape[1:]), 0, 1))

    f = np.zeros((TG, R + 1, NG, P), np.float32)
    tiled = g["edge_attr_20"].reshape(T, P, R)
    for t in range(T):
        f[t % TG, :R, t // TG] = tiled[t].T
    f[:, R] = 1.0
    w1 = np.zeros((TG, R + 1, TG, F), np.float32)
    w2 = np.zeros((TG, F, TG, 4, F), np.float32)
    order = [0, 3, 2, 1]
    w2k = g["L1_gnn_W2"].reshape(F, F, 6).transpose(0, 2, 1)[:, order]
    b2k = g["L1_gnn_b2"].reshape(F, 6).T[order].reshape(-1)
    for j in range(TG):
        w1[j, :R, j] = g["L1_gnn_W1"]
        w1[j, R, j] = g["L1_gnn_b1"]
        w2[j, :, j] = w2k
    b2 = np.zeros((96, 4 * F), np.float32)
    b2[0::32] = b2k
    bf = ml_dtypes.bfloat16
    eye = np.zeros((P, N // P, N), bf)
    for a in range(N // P):
        eye[:, a, a * P:(a + 1) * P] = np.eye(P, dtype=bf)
    o1v_t = np.ascontiguousarray(g["L1_gnn_w_f2o1_v"].T)
    arrays = {
        "x": g["x"],
        "idx": np.concatenate([edges_on_partitions(g["src"]), edges_on_partitions(g["dst"])], 1),
        "dst_row": g["dst"].reshape(1, E),
        "f_t": f.reshape(TG * (R + 1), NG * P),
        "yr": edges_on_partitions(g["edge_attr_4"]),
        "rcut": edges_on_partitions(g["edge_weight"]),
        "w0": g["L0_gnn_weight"],
        "bias0": g["L0_gnn_bias"].reshape(1, -1),
        "w1": w1.reshape(TG * (R + 1), TG * F),
        "w2": w2.reshape(TG * F, TG * 4 * F),
        "b2": b2,
        "w_in": np.concatenate([g["L1_gnn_w_in2f_s"], g["L1_gnn_w_in2f_v"]], 1),
        "w_o1s": g["L1_gnn_w_f2o1_s"],
        "w_o1vt": np.concatenate([o1v_t, o1v_t], 1),
        "w_o2s": g["L1_gnn_w_f2o2_s"],
        "w_o2v": g["L1_gnn_w_f2o2_v"],
        "ident": np.eye(P, dtype=np.float32),
        "iota_row": np.broadcast_to(np.arange(N), (P, N)).astype(bf),
        "iota_col": np.arange(N, dtype=np.float32).reshape(N // P, P).T,
        "eye2": eye,
    }
    arrays = {k: np.ascontiguousarray(v) for k, v in arrays.items()}
    nc = bacc.Bacc("TRN2", target_bir_lowering=False, num_devices=1)
    args = [nc.dram_tensor(k, v.shape, mybir.dt.from_np(v.dtype), kind="ExternalInput").ap() for k, v in arrays.items()]
    out = nc.dram_tensor("out", g["x"].shape, mybir.dt.float32, kind="ExternalOutput").ap()
    gnn_preln_kernel(nc, *args, out)
    r = run_bass_kernel_spmd(nc, [arrays], core_ids=[0])
    return r.results[0]["out"]
```

```python
import concourse.bass as bass
from concourse import mybir
from contextlib import ExitStack


def gnn_preln_kernel(nc, x, idx, dst_row, f_t, yr, w0, bias0, w1, w2, b2, w_in, w_o1s, w_o1vt, w_o2s, w_o2v,
                     iota_eye, ident_iota, out):
    fp32 = mybir.dt.float32
    fp32r = mybir.dt.float32r
    bf16 = mybir.dt.bfloat16
    i32 = mybir.dt.int32
    ALU = mybir.AluOpType
    ACT = mybir.ActivationFunctionType

    P = 128
    N, D = x.shape
    NH = N // P
    KD = D // P
    T = idx.shape[1] // 2
    E = T * P
    TG = 4
    NG = (T + TG - 1) // TG
    F = w1.shape[1] // TG
    B = w_in.shape[0]
    C = 4 * F
    S = 8
    KF = f_t.shape[0]
    RG = 3
    RW = 4
    POOL_FILTERS = (1, 3, 5)
    LATE = NG - 1
    WARM = 11
    PT = T - 4
    LN_EPS = 1e-5
    IS3 = 3.0 ** -0.5
    SB = B ** -0.5
    SF = (2 * F) ** -0.5

    def tiles(g):
        return min(TG, T - TG * g)

    ctx = ExitStack()
    with ctx:
        def sb(name, shape, dt=fp32):
            return ctx.enter_context(nc.sbuf_tensor(name, shape, dt))

        def sem(name):
            return ctx.enter_context(nc.semaphore(name))

        x_sb = sb("x_sb", [P, NH, D])
        idx_sb = sb("idx_sb", [P, 2 * T], i32)
        dst_bc = sb("dst_bc", [P, E], i32)
        f_sb = sb("f_sb", [KF, NG * P])
        yr_sb = sb("yr_sb", [P, T, 5])
        w0_sb = sb("w0_sb", [P, KD, D])
        b0_sb = sb("b0_sb", [P, D])
        w1_sb = sb("w1_sb", [KF, P])
        w2_sb = sb("w2_sb", [P, TG * P])
        b2_sb = sb("b2_sb", [96, P])
        win_sb = sb("win_sb", [B, 2 * F])
        o1s_sb = sb("o1s_sb", [2 * F, B])
        o1vt_sb = sb("o1vt_sb", [B, P])
        o2s_sb = sb("o2s_sb", [B, B])
        o2v_sb = sb("o2v_sb", [B, B])
        id_iota = sb("id_iota", [P, P + NH])
        id_sb, iota_c = id_iota[:, 0:P], id_iota[:, P:P + NH]
        ie_sb = sb("ie_sb", [P, 1 + NH, N], bf16)
        iota_r, eye_sb = ie_sb[:, 0, :], ie_sb[:, 1:1 + NH, :]
        idf = sb("idf", [P, 2 * T])
        idb = sb("idb", [P, P], bf16)
        dst_b = sb("dst_b", [P, E], bf16)
        Os = sb("Os", [P, T, N], bf16)
        onehot_dst = sb("onehot_dst", [P, T * N], bf16)
        Od = onehot_dst[:, :].rearrange("p (t n) -> p t n", t=T)
        OdT = onehot_dst[:, :].rearrange("p (a e) -> p a e", a=NH)
        OsR = sb("OsR", [P, RG, TG, N], fp32r)
        st6 = sb("st6", [P, NH, 6])
        mv1 = sb("mv1", [P, NH, 2])
        h1 = sb("h1", [P, NH, D])
        h1T = sb("h1T", [P, NH, KD, P])
        xb = sb("xb", [P, NH, D])
        ve = sb("ve", [P, NH])
        neghalf = sb("neghalf", [P, 2 * NH])
        CI = sb("CI", [P, NH, N], bf16)
        A = sb("A", [P, NH, N], fp32r)
        deg = sb("deg", [P, 2 * NH])
        scales = sb("scales", [P, 2 * NH])
        dinv, s1 = scales[:, 0:NH], scales[:, NH:2 * NH]
        hW_hi = sb("hW_hi", [P, NH, D], fp32r)
        hW_lo = sb("hW_lo", [P, NH, D], fp32r)
        x1 = sb("x1", [P, NH, D])
        xsum = sb("xsum", [P, NH])
        sq = sb("sq", [P, NH])
        h2, h2T = h1, h1T
        ve2 = sb("ve2", [P, NH])
        s2 = sb("s2", [P, NH])
        Hr = sb("Hr", [P, NH, C])
        Hp = [sb(f"Hp{i}", [P, NH, C], bf16) for i in range(3)]
        za = sb("za", [P, NG * P])
        hT = sb("hT", [P, NG * P])
        ones = sb("ones", [96, P], bf16)
        b2h = sb("b2h", [96, P], bf16)
        b2m = sb("b2m", [96, P], bf16)
        b2r = sb("b2r", [96, P])
        b2p = sb("b2p", [96, P], bf16)
        y = sb("y", [P, T, 4])
        Wsb = w0_sb
        warmup = sb("warmup", [P, 512], bf16)
        WY = sb("WY", [P, T, S * F])
        late = dst_bc[:].bitcast(fp32)
        M = late[:, 0:RG * TG * S * F].rearrange("p (o b t n) -> p o b t n", o=RG, b=2, t=TG)
        tmp = late[:, RG * TG * S * F:RG * TG * (S + 3) * F].rearrange("p (o t n) -> p o t n", o=RG, t=TG)
        Mh = sb("Mh", [P, RG, 2, TG, 4 * F], fp32r)
        Ml = sb("Ml", [P, RG, 2, TG, 4 * F], fp32r)
        aggT = sb("aggT", [P, 2, N])
        wc_sb = sb("wc_sb", [P, B])
        ta, te, te2, os1T = (za[:, i * N:(i + 1) * N] for i in range(4))
        o_sb = x_sb
        warm = sb("warm", [P, 1])

        bank = [ctx.enter_context(nc.psum_tensor(f"bank{i}", [P, 512], fp32)) for i in range(8)]
        bT = bank[2][:, :].bitcast(bf16)

        (d_x, d_idx, d_dst, d_f, d_yr, d_w0, d_b0, d_w1, d_w2, d_b2, d_win, d_o1s, d_o1v, d_o2s, d_o2v, d_id,
         d_ie, d_out) = [sem("dma_" + n) for n in
                         "x idx dst f yr w0 b0 w1 w2 b2 win o1s o1v o2s o2v id ie out".split()]
        names = ("half warmup idf idb st mv1 ve h1 tp1 h1T hW onehot onehot_p adj CI CT A degve scales hW_hi hW_hi1 hW_lo L0 xb x1 "
                 "h2 tp2 h2T sq ve2 s2 H Hp0 Hr Hp1 Hp2 z zabs zexp zln hT ones b2h b2r b2m b2p W Wsb y WYp WYd dstb OdT "
                 "OsR G prod part MA MB MhA MhB MlA MlB MlA_late MlB_late scat scatA aggA aggT wc wcs o1 os1 ta te tl rl os1T fin os2 ov o")
        q = {n: sem("s_" + n) for n in names.split()}

        zb = (bank[2], bank[3], bank[7])
        gbank = (bank[0], bank[1], bank[7])

        def weighted(g):
            own = [i for i in range(NG) if (i in POOL_FILTERS) == (g in POOL_FILTERS)]
            return q["WYp" if g in POOL_FILTERS else "WYd"], own.index(g) + 1

        def weight_filters(eng, wait_ge, g):
            t0, n = TG * g, tiles(g)
            w = Wsb[:, g % RW, 0:n * P].rearrange("p (t k f) -> p t k f", t=n, k=4)
            wy = WY[:, t0:t0 + n, :].rearrange("p t (k f) -> p t k f", k=S)
            yv = y[:, t0:t0 + n, 1:4].unsqueeze(3).broadcast_to((P, n, 3, F))
            y0 = y[:, t0:t0 + n, 0:1].unsqueeze(3).broadcast_to((P, n, 2, F))
            wait_ge(q["Wsb"], g + 1)
            wait_ge(q["y"], 1)
            eng.tensor_tensor(wy[:, :, 0:8:4, :], w[:, :, 0:2, :], y0, ALU.mult)
            eng.tensor_tensor(wy[:, :, 1:4, :], w[:, :, 2:3, :].broadcast_to((P, n, 3, F)), yv, ALU.mult)
            eng.tensor_tensor(wy[:, :, 5:8, :], w[:, :, 3:4, :].broadcast_to((P, n, 3, F)), yv,
                              ALU.mult).then_inc(weighted(g)[0], 1)

        block = ctx.enter_context(nc.Block())

        @block.sync
        def _(sp):
            sp.dma_start(idx_sb[:], idx).then_inc(d_idx, 16)
            sp.dma_start(w1_sb[:], w1).then_inc(d_w1, 16)
            sp.dma_start(x_sb[:, :, :], x.rearrange("(a p) d -> p a d", p=P)).then_inc(d_x, 16)
            sp.dma_start(w0_sb[:, :, :], w0.rearrange("(k p) n -> p k n", p=P)).then_inc(d_w0, 16)
            sp.dma_start(b0_sb[:], bias0.broadcast_to((P, D))).then_inc(d_b0, 16)
            sp.dma_start(win_sb[:], w_in).then_inc(d_win, 16)
            sp.dma_start(o1s_sb[:], w_o1s).then_inc(d_o1s, 16)
            sp.dma_start(dst_bc[:], dst_row.broadcast_to((P, E))).then_inc(d_dst, 16)
            sp.dma_start(o1vt_sb[:], w_o1vt).then_inc(d_o1v, 16)
            sp.dma_start(o2s_sb[:], w_o2s).then_inc(d_o2s, 16)
            sp.dma_start(o2v_sb[:], w_o2v).then_inc(d_o2v, 16)
            for a in range(NH):
                sp.wait_ge(q["ov"], a + 1)
                sp.dma_start(out[a * P:(a + 1) * P, B:], o_sb[:, a, B:]).then_inc(d_out, 16)
            sp.wait_ge(d_out, 16 * (NH + 1))

        @block.scalar
        def _(act):
            act.dma_start(ie_sb[:, :, :], iota_eye).then_inc(d_ie, 16)
            act.dma_start(f_sb[:], f_t).then_inc(d_f, 16)
            act.dma_start(id_iota[:], ident_iota).then_inc(d_id, 16)
            act.dma_start(w2_sb[:], w2).then_inc(d_w2, 16)
            act.dma_start(b2_sb[:], b2).then_inc(d_b2, 16)
            act.dma_start(yr_sb[:, :, :], yr).then_inc(d_yr, 16)
            nc.scalar.preload_act_table_set("natural_log_exp_and_others")
            for c in range(3):
                lo, hi = 512 * c, min(512 * (c + 1), NG * P)
                act.wait_ge(q["z"], c + 1)
                nc.scalar.activation(za[:, lo:hi], zb[c][:, 0:hi - lo], ACT.Abs).then_inc(q["zabs"], 1)
            for a in range(NH):
                act.wait_ge(q["tp1"], a + 1)
                nc.scalar.activation(h1T[:, a, :, :], bank[(6, 1)[a]][:, :], ACT.Copy).then_inc(q["h1T"], 1)
            act.wait_ge(q["zabs"], 3)
            nc.scalar.activation(za[:], za[:], ACT.Exp, scale=-1.0).then_inc(q["zexp"], 1)
            act.wait_ge(q["zexp"], 1)
            act.wait_ge(q["half"], 1)
            nc.scalar.activation(za[:], za[:], ACT.Ln, bias=warm[:, 0:1], scale=0.5).then_inc(q["zln"], 1)
            act.wait_ge(d_dst, 16)
            nc.scalar.activation(dst_b[:], dst_bc[:], ACT.Copy).then_inc(q["dstb"], 1)

            def scatter_onehots(g):
                t0, n = TG * g, tiles(g)
                act.wait_ge(q["onehot"], 2 * min(t0 + n, PT))
                if t0 + n > PT:
                    act.wait_ge(q["onehot_p"], 2 * (t0 + n - PT))
                if g >= RG:
                    act.wait_ge(q["scat"], g - RG + 1)
                nc.scalar.activation(OsR[:, g % RG, 0:n, :], Os[:, t0:t0 + n, :], ACT.Copy).then_inc(q["OsR"], 1)

            for g in range(RG):
                scatter_onehots(g)

            def filters_out(g):
                act.wait_ge(q["W"], g + 1)
                if g == 0:
                    act.wait_ge(q["hW"], NH)
                if g >= RW:
                    act.wait_ge(*weighted(g - RW))
                n = tiles(g)
                nc.scalar.activation(Wsb[:, g % RW, 0:n * P], bank[3 - g % 2][:, 0:n * P], ACT.Copy).then_inc(q["Wsb"], 1)

            filters_out(0)
            act.wait_ge(q["scales"], 1)
            nc.scalar.activation(hW_hi[:, 0, :], bank[0][:, :], ACT.Copy, scale=s1[:, 0:1]).then_inc(q["hW_hi"], 1)
            for g in range(1, 4):
                filters_out(g)
            act.wait_ge(q["h2"], 1)
            nc.scalar.activation(za[:, 0:D], h2[:, 0, :], ACT.Square, accum_out=sq[:, 0:1]).then_inc(q["sq"], 1)
            act.wait_ge(q["tp2"], 1)
            nc.scalar.activation(h2T[:, 0, :, :], bank[6][:, :], ACT.Relu).then_inc(q["h2T"], 1)
            act.wait_ge(q["h2"], 2)
            act.wait_ge(q["sq"], 1)
            nc.scalar.activation(za[:, 0:D], h2[:, 1, :], ACT.Square, accum_out=sq[:, 1:2]).then_inc(q["sq"], 1)
            for g in range(4, NG):
                filters_out(g)
            for g in range(NG):
                n = tiles(g)
                o = g % RG
                act.wait_ge(q["MB"], g + 1)
                if g >= RG:
                    act.wait_ge(q["scat"], g - RG + 1)
                nc.scalar.activation(Mh[:, o, 1, 0:n, :], M[:, o, 1, 0:n, :], ACT.Copy).then_inc(q["MhB"], 1)
                act.wait_ge(q["MA"], g + 1)
                nc.scalar.activation(Mh[:, o, 0, 0:n, :], M[:, o, 0, 0:n, :], ACT.Copy).then_inc(q["MhA"], 1)
                if g == 1:
                    act.wait_ge(q["wc"], 1)
                    nc.scalar.activation(wc_sb[:], bank[6][:, 0:B], ACT.Copy, scale=SF * SB).then_inc(q["wcs"], 1)
                if 1 <= g and g + RG - 1 < NG:
                    scatter_onehots(g + RG - 1)
            act.wait_ge(q["scat"], NG)
            nc.scalar.activation(aggT[:, 1, :], bank[5][:, 0:N], ACT.Copy).then_inc(q["aggT"], 1)
            act.wait_ge(q["os1"], 1)
            nc.scalar.activation(ta[:], bank[2][:, 0:N], ACT.Abs, scale=SF).then_inc(q["ta"], 1)
            act.wait_ge(q["ta"], 1)
            nc.scalar.activation(te[:], ta[:], ACT.Exp, scale=-1.0).then_inc(q["te"], 1)
            act.wait_ge(q["te"], 1)
            nc.scalar.activation(ta[:], te[:], ACT.Ln, bias=warm[:, 0:1], scale=0.5).then_inc(q["tl"], 1)
            act.wait_ge(q["o"], NH)
            act.dma_start(out.rearrange("(a p) d -> p a d", p=P)[:, :, 0:B], o_sb[:, :, 0:B]).then_inc(d_out, 16)

        @block.gpsimd
        def _(pool):
            nc.gpsimd.memset(warm[:], 0.5).then_inc(q["half"], 1)
            nc.gpsimd.memset(neghalf[:], -0.5).then_inc(q["half"], 1)
            nc.gpsimd.memset(ones[:], 1.0).then_inc(q["ones"], 1)
            pool.wait_ge(d_ie, 16)
            pool.wait_ge(q["idf"], 1)
            for t in range(PT, T):
                nc.gpsimd.tensor_scalar(Os[:, t, :], iota_r, idf[:, t:t + 1], None, ALU.is_equal).then_inc(q["onehot_p"], 1)
                nc.gpsimd.tensor_scalar(Od[:, t, :], iota_r, idf[:, T + t:T + t + 1], None,
                                        ALU.is_equal).then_inc(q["onehot_p"], 1)
            pool.wait_ge(d_b2, 16)
            nc.gpsimd.tensor_copy(b2h[:], b2_sb[:]).then_inc(q["b2h"], 1)
            pool.wait_ge(q["b2h"], 1)
            nc.gpsimd.tensor_tensor(b2r[:], b2_sb[:], b2h[:], ALU.subtract).then_inc(q["b2r"], 1)
            pool.wait_ge(q["b2r"], 1)
            nc.gpsimd.tensor_copy(b2m[:], b2r[:]).then_inc(q["b2m"], 1)
            pool.wait_ge(q["b2m"], 1)
            nc.gpsimd.tensor_copy(b2p[0:32, :], b2h[0:32, :]).then_inc(q["b2p"], 1)
            pool.wait_ge(q["b2p"], 1)
            nc.gpsimd.tensor_copy(b2p[32:64, :], b2m[32:64, :]).then_inc(q["b2p"], 1)
            pool.wait_ge(q["b2p"], 2)
            nc.gpsimd.tensor_tensor(b2p[64:96, :], b2r[64:96, :], b2m[64:96, :], ALU.subtract).then_inc(q["b2p"], 1)
            pool.wait_ge(q["b2p"], 3)
            pool.wait_ge(d_yr, 16)
            nc.gpsimd.tensor_tensor(y[:, :, :], yr_sb[:, :, 0:4], yr_sb[:, :, 4:5].broadcast_to((P, T, 4)),
                                    ALU.mult).then_inc(q["y"], 1)
            pool.wait_ge(d_b0, 16)
            pool.wait_ge(d_x, 16)
            nc.gpsimd.tensor_tensor(xb[:, :, :], x_sb[:, :, :], b0_sb[:].unsqueeze(1).broadcast_to((P, NH, D)),
                                    ALU.add).then_inc(q["xb"], 1)

            pool.wait_ge(q["degve"], 1)
            pool.wait_ge(q["half"], 2)
            nc.gpsimd.tensor_tensor(scales[:], deg[:], neghalf[:], ALU.pow).then_inc(q["scales"], 1)
            weight_filters(nc.gpsimd, pool.wait_ge, 1)
            weight_filters(nc.gpsimd, pool.wait_ge, 3)
            pool.wait_ge(q["sq"], NH)
            nc.gpsimd.tensor_scalar(ve2[:], sq[:], B / D, LN_EPS * D * D * B, ALU.mult, ALU.add).then_inc(q["ve2"], 1)
            pool.wait_ge(q["ve2"], 1)
            nc.gpsimd.tensor_tensor(s2[:], ve2[:], neghalf[:, 0:NH], ALU.pow).then_inc(q["s2"], 1)
            weight_filters(nc.gpsimd, pool.wait_ge, 5)
            for g in range(LATE):
                n = tiles(g)
                o = g % RG
                pool.wait_ge(q["MhB"], g + 1)
                if g >= RG:
                    pool.wait_ge(q["scat"], g - RG + 1)
                nc.gpsimd.tensor_tensor(Ml[:, o, 1, 0:n, :], M[:, o, 1, 0:n, :], Mh[:, o, 1, 0:n, :].bitcast(fp32),
                                        ALU.subtract).then_inc(q["MlB"], 1)
                pool.wait_ge(q["MhA"], g + 1)
                nc.gpsimd.tensor_tensor(Ml[:, o, 0, 0:n, :], M[:, o, 0, 0:n, :], Mh[:, o, 0, 0:n, :].bitcast(fp32),
                                        ALU.subtract).then_inc(q["MlA"], 1)

        @block.vector
        def _(dve):
            def onehots(t0, t1):
                for t in range(t0, t1):
                    nc.vector.tensor_scalar(Os[:, t, :], iota_r, idf[:, t:t + 1], None, ALU.is_equal).then_inc(q["onehot"], 1)
                    nc.vector.tensor_scalar(Od[:, t, :], iota_r, idf[:, T + t:T + t + 1], None,
                                            ALU.is_equal).then_inc(q["onehot"], 1)

            nc.vector.memset(warmup[:], 0.0).then_inc(q["warmup"], 1)
            dve.wait_ge(d_idx, 16)
            nc.vector.tensor_copy(idf[:], idx_sb[:]).then_inc(q["idf"], 1)
            dve.wait_ge(q["idf"], 1)
            dve.wait_ge(d_ie, 16)
            onehots(0, 6)
            dve.wait_ge(d_x, 16)
            for a in range(NH):
                nc.vector.bn_stats(st6[:, a, :], x_sb[:, a, :]).then_inc(q["st"], 1)
            for a in range(NH):
                dve.wait_ge(q["st"], a + 1)
                nc.vector.bn_aggr(mv1[:, a, :], st6[:, a, :]).then_inc(q["mv1"], 1)
            for a in range(NH):
                dve.wait_ge(q["mv1"], a + 1)
                nc.vector.tensor_scalar(h1[:, a, :], x_sb[:, a, :], mv1[:, a, 0:1], 0.0, ALU.subtract,
                                        ALU.max).then_inc(q["h1"], 1)
            nc.vector.tensor_scalar(ve[:], mv1[:, :, 1], LN_EPS, None, ALU.add).then_inc(q["ve"], 1)
            onehots(6, 16)
            dve.wait_ge(q["zln"], 1)
            for c in range(3):
                lo, hi = 512 * c, min(512 * (c + 1), NG * P)
                nc.vector.scalar_tensor_tensor(hT[:, lo:hi], zb[c][:, 0:hi - lo], 0.0, za[:, lo:hi],
                                               ALU.max, ALU.add).then_inc(q["hT"], 1)
            onehots(16, PT)
            dve.wait_ge(d_id, 16)
            nc.vector.tensor_copy(idb[:], id_sb).then_inc(q["idb"], 1)
            dve.wait_ge(d_o1s, 16)
            nc.vector.tensor_scalar(o1s_sb[F:2 * F, :], o1s_sb[F:2 * F, :], IS3, None, ALU.mult).then_inc(q["o1"], 1)
            dve.wait_ge(q["adj"], 1)
            for a in range(NH):
                nc.vector.scalar_tensor_tensor(CI[:, a, :], bank[4 + a][:, 0:N], 1.0, eye_sb[:, a, :], ALU.min,
                                               ALU.add).then_inc(q["CI"], 1)
            dve.wait_ge(q["CT"], 1)
            for a in range(NH):
                dve.wait_ge(q["CI"], a + 1)
                nc.vector.scalar_tensor_tensor(A[:, a, :], bT[:, a * N:(a + 1) * N], 0.0, CI[:, a, :], ALU.add,
                                               ALU.max, accum_out=deg[:, a:a + 1]).then_inc(q["A"], 1)
            dve.wait_ge(q["A"], NH)
            dve.wait_ge(q["ve"], 1)
            nc.vector.tensor_tensor(deg[:, NH:2 * NH], deg[:, 0:NH], ve[:], ALU.mult).then_inc(q["degve"], 1)

            def node_onehots(a, c):
                lo, hi = c * E // 2, (c + 1) * E // 2
                nc.vector.tensor_scalar(OdT[:, a, lo:hi], dst_b[:, lo:hi], iota_c[:, a:a + 1], None,
                                        ALU.is_equal).then_inc(q["OdT"], 1)

            weight_filters(nc.vector, dve.wait_ge, 0)
            dve.wait_ge(q["scales"], 1)
            nc.vector.tensor_scalar(hW_hi[:, 1, :], bank[1][:, :], s1[:, 1:2], None, ALU.mult).then_inc(q["hW_hi1"], 1)
            for a in range(NH):
                dve.wait_ge(q[("hW_hi", "hW_hi1")[a]], 1)
                nc.vector.scalar_tensor_tensor(hW_lo[:, a, :], bank[a][:, :], s1[:, a:a + 1],
                                               hW_hi[:, a, :].bitcast(fp32), ALU.mult, ALU.subtract).then_inc(q["hW_lo"], 1)
            dve.wait_ge(q["dstb"], 1)
            node_onehots(0, 0)
            node_onehots(1, 0)
            dve.wait_ge(q["xb"], 1)
            for a in range(NH):
                dve.wait_ge(q["L0"], a + 1)
                nc.vector.scalar_tensor_tensor(x1[:, a, :], bank[a][:, :], dinv[:, a:a + 1], xb[:, a, :], ALU.mult,
                                               ALU.add, accum_out=xsum[:, a:a + 1]).then_inc(q["x1"], 1)
                dve.wait_ge(q["x1"], a + 1)
                nc.vector.tensor_scalar(h2[:, a, :], x1[:, a, :], float(D), xsum[:, a:a + 1], ALU.mult,
                                        ALU.subtract).then_inc(q["h2"], 1)

            dve.wait_ge(q["tp2"], 2)
            nc.vector.tensor_scalar(h2T[:, 1, :, :], bank[7][:, :].rearrange("p (k n) -> p k n", k=KD), 0.0, None,
                                    ALU.max).then_inc(q["h2T"], 1)
            weight_filters(nc.vector, dve.wait_ge, 2)
            dve.wait_ge(q["s2"], 1)
            dve.wait_ge(q["H"], 1)
            for a in range(NH):
                nc.vector.tensor_scalar(Hp[0][:, a, :], bank[6][:, a * C:(a + 1) * C], s2[:, a:a + 1], None,
                                        ALU.mult).then_inc(q["Hp0"], 1)
            for a in range(NH):
                dve.wait_ge(q["Hp0"], a + 1)
                nc.vector.scalar_tensor_tensor(Hr[:, a, :], bank[6][:, a * C:(a + 1) * C], s2[:, a:a + 1], Hp[0][:, a, :],
                                               ALU.mult, ALU.subtract).then_inc(q["Hr"], 1)
            dve.wait_ge(q["Hr"], NH)
            nc.vector.tensor_copy(Hp[1][:, :, :], Hr[:, :, :]).then_inc(q["Hp1"], 1)
            dve.wait_ge(q["Hp1"], 1)
            nc.vector.tensor_tensor(Hp[2][:, :, :], Hr[:, :, :], Hp[1][:, :, :], ALU.subtract).then_inc(q["Hp2"], 1)
            weight_filters(nc.vector, dve.wait_ge, 4)
            for g in range(NG):
                t0, n, o = TG * g, tiles(g), g % RG
                G = gbank[o][:, 0:n * C].rearrange("p (t c f) -> p t c f", t=n, c=4)
                wy = WY[:, t0:t0 + n, :].rearrange("p t (k f) -> p t k f", k=S)
                mA, mB = (M[:, o, b, 0:n, :].rearrange("p t (k f) -> p t k f", k=4) for b in range(2))
                tc = tmp[:, o, 0:n, :].rearrange("p t (c f) -> p t c f", c=3)
                dve.wait_ge(q["G"], g + 1)
                dve.wait_ge(*weighted(g))
                if g >= RG:
                    dve.wait_ge(q["MlA"], g - RG + 1)
                sn = G[:, :, 0:1, :]
                nc.vector.tensor_tensor(mB[:, :, 0:4:2, :], sn.broadcast_to((P, n, 2, F)), wy[:, :, 2:4, :], ALU.mult)
                nc.vector.tensor_tensor(mB[:, :, 1:4:2, :], G[:, :, 2:4, :], wy[:, :, 4:5, :].broadcast_to((P, n, 2, F)),
                                        ALU.mult).then_inc(q["MB"], 1)
                nc.vector.tensor_tensor(tc, G[:, :, 1:4, :], wy[:, :, 5:8, :], ALU.mult).then_inc(q["part"], 1)
                nc.vector.tensor_tensor(mA[:, :, 0:4:2, :], sn.broadcast_to((P, n, 2, F)), wy[:, :, 0:2, :], ALU.mult)
                nc.vector.tensor_tensor(mA[:, :, 3, :], G[:, :, 1, :], wy[:, :, 4, :], ALU.mult).then_inc(q["prod"], 1)
                dve.wait_ge(q["part"], g + 1)
                nc.vector.tensor_reduce(mA[:, :, 1, :], tc.rearrange("p t c f -> p t f c"), mybir.AxisListType.X,
                                        ALU.add).then_inc(q["MA"], 1)
                if 1 <= g <= NH:
                    node_onehots(g - 1, 1)
                elif g + 3 in (6, 7, 8):
                    weight_filters(nc.vector, dve.wait_ge, g + 3)
            for b, high, low in ((0, "MhA", "MlA_late"), (1, "MhB", "MlB_late")):
                o, n = LATE % RG, tiles(LATE)
                dve.wait_ge(q[high], LATE + 1)
                nc.vector.tensor_tensor(Ml[:, o, b, 0:n, :], M[:, o, b, 0:n, :], Mh[:, o, b, 0:n, :].bitcast(fp32),
                                        ALU.subtract).then_inc(q[low], 1)
            dve.wait_ge(q["scatA"], 1)
            nc.vector.tensor_copy(aggT[:, 0, :], bank[4][:, 0:N]).then_inc(q["aggA"], 1)
            dve.wait_ge(q["ta"], 1)
            nc.vector.tensor_scalar(te2[:], bank[2][:, 0:N], SF, 0.0, ALU.mult, ALU.max).then_inc(q["rl"], 1)
            for a in range(NH):
                dve.wait_ge(q["fin"], a + 1)
                ov = o_sb[:, a, B:].rearrange("p (d c) -> p c d", c=3)
                xv = x1[:, a, B:].rearrange("p (d c) -> p c d", c=3)
                xz = bank[a][:, 0:2 * B].rearrange("p (c d) -> p c d", c=2)
                nc.vector.tensor_tensor(ov[:, 0:3:2, :], xz, xv[:, 0:3:2, :], ALU.add)
                nc.vector.tensor_tensor(ov[:, 1, :], bank[6 + a][:, 0:B], xv[:, 1, :], ALU.add).then_inc(q["ov"], 1)
                if a == 0:
                    dve.wait_ge(q["tl"], 1)
                    dve.wait_ge(q["rl"], 1)
                    nc.vector.tensor_tensor(os1T[:], te2[:], ta[:], ALU.add).then_inc(q["os1T"], 1)
            for a in range(NH):
                dve.wait_ge(q["os2"], a + 1)
                nc.vector.scalar_tensor_tensor(o_sb[:, a, 0:B], bank[2 + a][:, 0:B], SB, x1[:, a, 0:B], ALU.mult,
                                               ALU.add).then_inc(q["o"], 1)

        @block.tensor
        def _(pe):
            pe.wait_ge(q["warmup"], 1)
            for _ in range(WARM):
                nc.tensor.matmul(bank[0][:, :], warmup[:, 0:P], warmup[:], start=True, stop=True)
            pe.wait_ge(d_f, 16)
            pe.wait_ge(d_w1, 16)
            for c in range(3):
                lo, hi = 512 * c, min(512 * (c + 1), NG * P)
                nc.tensor.matmul(zb[c][:, 0:hi - lo], w1_sb[:], f_sb[:, lo:hi], start=True, stop=True).then_inc(q["z"], 1)
            pe.wait_ge(d_id, 16)
            for a in range(NH):
                pe.wait_ge(q["h1"], a + 1)
                for k in range(KD):
                    last = nc.tensor.transpose(bank[(6, 1)[a]][:, k * P:(k + 1) * P], h1[:, a, k * P:(k + 1) * P], id_sb)
                last.then_inc(q["tp1"], 1)
            pe.wait_ge(d_w0, 16)
            for a in range(NH):
                pe.wait_ge(q["h1T"], a + 1)
                for k in range(KD):
                    last = nc.tensor.matmul(bank[a][:, :], h1T[:, a, k, :], w0_sb[:, k, :], start=(k == 0), stop=(k == KD - 1))
                last.then_inc(q["hW"], 1)

            def adjacency(t0, t1):
                for t in range(t0, t1):
                    if t < PT:
                        pe.wait_ge(q["onehot"], 2 * t + 2)
                    else:
                        pe.wait_ge(q["onehot_p"], 2 * (t - PT) + 2)
                    for a in range(NH):
                        last = nc.tensor.matmul(bank[4 + a][:, 0:N], Os[:, t, a * P:(a + 1) * P], Od[:, t, :],
                                                start=(t == 0), stop=(t == T - 1))
                if t1 == T:
                    last.then_inc(q["adj"], 1)

            def filters(g):
                n = tiles(g)
                k = 32 * n
                if g == 0:
                    pe.wait_ge(q["hT"], 3)
                    pe.wait_ge(d_w2, 16)
                    pe.wait_ge(q["b2p"], 3)
                    pe.wait_ge(q["ones"], 1)
                if g == 1:
                    pe.wait_ge(q["A"], NH)
                if g >= 2:
                    pe.wait_ge(q["Wsb"], g - 1)
                ps = bank[3 - g % 2][:, 0:n * P]
                nc.tensor.matmul(ps, ones[:], b2p[:].unsqueeze(1).broadcast_to((96, n, P)), start=True, stop=False)
                nc.tensor.matmul(ps, hT[0:k, g * P:(g + 1) * P], w2_sb[0:k, 0:n * P], start=False, stop=True).then_inc(q["W"], 1)

            adjacency(0, T)
            filters(0)
            pe.wait_ge(q["idb"], 1)
            pe.wait_ge(q["CI"], NH)
            for a in range(NH):
                for b in range(NH):
                    last = nc.tensor.transpose(bT[:, a * N + b * P:a * N + (b + 1) * P], CI[:, b, a * P:(a + 1) * P], idb[:])
            last.then_inc(q["CT"], 1)
            filters(1)
            filters(2)
            filters(3)
            for a in range(NH):
                for b in range(NH):
                    if a == 0:
                        pe.wait_ge(q["hW_lo"], NH)
                    for part in (hW_hi, hW_lo):
                        last = nc.tensor.matmul(bank[a][:, :], A[:, b, a * P:(a + 1) * P], part[:, b, :],
                                                start=(b == 0 and part is hW_hi), stop=(b == NH - 1 and part is hW_lo))
                last.then_inc(q["L0"], 1)
            filters(4)
            for a in range(NH):
                pe.wait_ge(q["h2"], a + 1)
                for k in range(4):
                    src = h2[:, a, 0:B] if k == 0 else h2[:, a, B:].rearrange("p (b c) -> p c b", c=3)[:, k - 1, :]
                    last = nc.tensor.transpose(bank[6 + a][:, k * P:(k + 1) * P], src, id_sb)
                last.then_inc(q["tp2"], 1)
            filters(5)
            pe.wait_ge(d_win, 16)
            pe.wait_ge(q["h2T"], NH)
            for a in range(NH):
                for k in range(4):
                    w = win_sb[:, 0:F] if k == 0 else win_sb[:, F:2 * F]
                    last = nc.tensor.matmul(bank[6][:, a * C + k * F:a * C + (k + 1) * F], h2T[:, a, k, :], w,
                                            start=True, stop=True)
            last.then_inc(q["H"], 1)
            filters(6)
            filters(7)

            def gather(g):
                if g == 0:
                    pe.wait_ge(q["OdT"], NH)
                    pe.wait_ge(q["Hp2"], 1)
                if (TG * g + tiles(g)) * P > E // 2:
                    pe.wait_ge(q["OdT"], 2 * NH)
                if g >= RG:
                    pe.wait_ge(q["prod"], g - RG + 1)
                for j in range(tiles(g)):
                    t = TG * g + j
                    for a in range(NH):
                        for i in range(3):
                            last = nc.tensor.matmul(gbank[g % RG][:, j * C:(j + 1) * C], OdT[:, a, t * P:(t + 1) * P],
                                                    Hp[i][:, a, :], start=(a == 0 and i == 0), stop=(a == NH - 1 and i == 2))
                last.then_inc(q["G"], 1)

            def scatter(g):
                pe.wait_ge(q["OsR"], g + 1)
                for b in (1, 0) if g < LATE else (0, 1):
                    if g < LATE:
                        pe.wait_ge(q[("MlA", "MlB")[b]], g + 1)
                    else:
                        pe.wait_ge(q[("MlA_late", "MlB_late")[b]], 1)
                    for j in range(tiles(g)):
                        t = TG * g + j
                        for part in (Mh, Ml):
                            last = nc.tensor.matmul(bank[4 + b][:, 0:N], part[:, g % RG, b, j, :], OsR[:, g % RG, j, :],
                                                    start=(t == 0 and part is Mh), stop=(t == T - 1 and part is Ml))
                    if g == LATE and b == 0:
                        last.then_inc(q["scatA"], 1)
                last.then_inc(q["scat"], 1)

            LAG = 2
            for g in range(NG + LAG):
                if g < NG:
                    gather(g)
                    if g + 8 < NG:
                        filters(g + 8)
                if g == LAG:
                    pe.wait_ge(d_o1v, 16)
                    pe.wait_ge(d_o2v, 16)
                    nc.tensor.matmul(bank[6][:, 0:B], o1vt_sb[:], o2v_sb[:], start=True, stop=True).then_inc(q["wc"], 1)
                if g >= LAG:
                    scatter(g - LAG)
            pe.wait_ge(q["aggA"], 1)
            pe.wait_ge(q["o1"], 1)
            nc.tensor.matmul(bank[2][:, 0:N], o1s_sb[:], aggT[0:64, 0, :], start=True, stop=True).then_inc(q["os1"], 1)
            pe.wait_ge(q["aggT"], 1)
            pe.wait_ge(q["wcs"], 1)
            pe.wait_ge(d_o2s, 16)
            for a in range(NH):
                n = slice(a * P, (a + 1) * P)
                nc.tensor.matmul(bank[a][:, 0:B], aggT[64:128, 0, n], wc_sb[64:128, :], start=True, stop=True)
                nc.tensor.matmul(bank[a][:, B:2 * B], aggT[64:128, 1, n], wc_sb[64:128, :], start=True, stop=True)
                nc.tensor.matmul(bank[6 + a][:, 0:B], aggT[0:64, 1, n], wc_sb[0:64, :], start=True,
                                 stop=True).then_inc(q["fin"], 1)
            pe.wait_ge(q["os1T"], 1)
            for a in range(NH):
                n = slice(a * P, (a + 1) * P)
                nc.tensor.matmul(bank[2 + a][:, 0:B], os1T[:, n], o2s_sb[:], start=True, stop=True).then_inc(q["os2"], 1)


def kernel(x, src, dst, edge_attr_20, edge_attr_4, edge_weight, L0_gnn_weight, L0_gnn_bias, L1_gnn_w_in2f_s,
           L1_gnn_w_in2f_v, L1_gnn_W1, L1_gnn_b1, L1_gnn_W2, L1_gnn_b2, L1_gnn_w_f2o1_s, L1_gnn_w_f2o1_v,
           L1_gnn_w_f2o2_s, L1_gnn_w_f2o2_v):
    import ml_dtypes
    import numpy as np
    import concourse.bacc as bacc
    from concourse.bass_utils import run_bass_kernel_spmd

    g = {k: np.asarray(v) for k, v in locals().items() if isinstance(v, object) and hasattr(v, "shape")}
    P, TG = 128, 4
    E, R = g["edge_attr_20"].shape
    F = g["L1_gnn_W1"].shape[1]
    T = E // P
    NG = -(-T // TG)
    N = g["x"].shape[0]

    def edges_on_partitions(a):
        return np.ascontiguousarray(np.moveaxis(a.reshape(T, P, *a.shape[1:]), 0, 1))

    f = np.zeros((TG, R + 1, NG, P), np.float32)
    tiled = g["edge_attr_20"].reshape(T, P, R)
    for t in range(T):
        f[t % TG, :R, t // TG] = tiled[t].T
    f[:, R] = 1.0
    w1 = np.zeros((TG, R + 1, TG, F), np.float32)
    w2 = np.zeros((TG, F, TG, 4, F), np.float32)
    order = [0, 3, 2, 1]
    w2k = g["L1_gnn_W2"].reshape(F, F, 6).transpose(0, 2, 1)[:, order]
    b2k = g["L1_gnn_b2"].reshape(F, 6).T[order].reshape(-1)
    for j in range(TG):
        w1[j, :R, j] = g["L1_gnn_W1"]
        w1[j, R, j] = g["L1_gnn_b1"]
        w2[j, :, j] = w2k
    b2 = np.zeros((96, 4 * F), np.float32)
    b2[0::32] = b2k
    bf = ml_dtypes.bfloat16
    iota_eye = np.zeros((P, 1 + N // P, N), bf)
    iota_eye[:, 0] = np.arange(N)
    for a in range(N // P):
        iota_eye[:, 1 + a, a * P:(a + 1) * P] = np.eye(P, dtype=bf)
    o1v_t = np.ascontiguousarray(g["L1_gnn_w_f2o1_v"].T)
    arrays = {
        "x": g["x"],
        "idx": np.concatenate([edges_on_partitions(g["src"]), edges_on_partitions(g["dst"])], 1),
        "dst_row": g["dst"].reshape(1, E),
        "f_t": f.reshape(TG * (R + 1), NG * P),
        "yr": np.concatenate([edges_on_partitions(g["edge_attr_4"]), edges_on_partitions(g["edge_weight"])[..., None]], 2),
        "w0": g["L0_gnn_weight"],
        "bias0": g["L0_gnn_bias"].reshape(1, -1),
        "w1": w1.reshape(TG * (R + 1), TG * F),
        "w2": w2.reshape(TG * F, TG * 4 * F),
        "b2": b2,
        "w_in": np.concatenate([g["L1_gnn_w_in2f_s"], g["L1_gnn_w_in2f_v"]], 1),
        "w_o1s": g["L1_gnn_w_f2o1_s"],
        "w_o1vt": np.concatenate([o1v_t, o1v_t], 1),
        "w_o2s": g["L1_gnn_w_f2o2_s"],
        "w_o2v": g["L1_gnn_w_f2o2_v"],
        "iota_eye": iota_eye,
        "ident_iota": np.concatenate([np.eye(P, dtype=np.float32), np.arange(N, dtype=np.float32).reshape(N // P, P).T], 1),
    }
    arrays = {k: np.ascontiguousarray(v) for k, v in arrays.items()}
    nc = bacc.Bacc("TRN2", target_bir_lowering=False, num_devices=1)
    args = [nc.dram_tensor(k, v.shape, mybir.dt.from_np(v.dtype), kind="ExternalInput").ap() for k, v in arrays.items()]
    out = nc.dram_tensor("out", g["x"].shape, mybir.dt.float32, kind="ExternalOutput").ap()
    gnn_preln_kernel(nc, *args, out)
    r = run_bass_kernel_spmd(nc, [arrays], core_ids=[0])
    return r.results[0]["out"]
```

```python
import concourse.bass as bass
from concourse import mybir
from contextlib import ExitStack


def gnn_preln_kernel(nc, x, idx, dst_row, f_t, yr, w0, bias0, w1, w2, b2, w_in, w_o1s, w_o1vt, w_o2s, w_o2v,
                     eye, ident_iota, out):
    fp32 = mybir.dt.float32
    fp32r = mybir.dt.float32r
    bf16 = mybir.dt.bfloat16
    i32 = mybir.dt.int32
    ALU = mybir.AluOpType
    ACT = mybir.ActivationFunctionType

    P = 128
    N, D = x.shape
    NH = N // P
    KD = D // P
    T = dst_row.shape[1] // P
    E = T * P
    TG = 4
    NG = (T + TG - 1) // TG
    F = w1.shape[1] // TG
    B = w_in.shape[0]
    C = 4 * F
    S = 8
    KF = f_t.shape[0]
    RG = 3
    RW = 4
    POOL_FILTERS = (0, 1, 3, 4)
    LATE = NG - 1
    WARM = 8
    PT = T - 7
    LN_EPS = 1e-5
    IS3 = 3.0 ** -0.5
    SB = B ** -0.5
    SF = (2 * F) ** -0.5


    def tiles(g):
        return min(TG, T - TG * g)

    ctx = ExitStack()
    with ctx:
        def sb(name, shape, dt=fp32):
            return ctx.enter_context(nc.sbuf_tensor(name, shape, dt))

        def sem(name):
            return ctx.enter_context(nc.semaphore(name))

        x_sb = sb("x_sb", [P, NH, D])
        idx_sb = sb("idx_sb", [P, 2 * T + N], i32)
        dst_bc = sb("dst_bc", [P, E], i32)
        f_sb = sb("f_sb", [KF, NG * P])
        yr_sb = sb("yr_sb", [P, T, 5])
        w0_sb = sb("w0_sb", [P, KD, D])
        b0_sb = sb("b0_sb", [P, D])
        w1_sb = sb("w1_sb", [KF, P])
        w2_sb = sb("w2_sb", [P, 2 * P])
        w2_hi = sb("w2_hi", [P, 2 * P], fp32r)
        w2_lo = sb("w2_lo", [P, 2 * P], fp32r)
        b2_sb = sb("b2_sb", [96, P])
        win_sb = sb("win_sb", [B, 2 * F])
        o1s_sb = sb("o1s_sb", [2 * F, B])
        o1vt_sb = sb("o1vt_sb", [B, P])
        o2s_sb = sb("o2s_sb", [B, B])
        o2v_sb = sb("o2v_sb", [B, B])
        id_iota = sb("id_iota", [P, P + NH])
        id_sb, iota_c = id_iota[:, 0:P], id_iota[:, P:P + NH]
        eye_sb = sb("eye_sb", [P, NH, N], bf16)

        idf = sb("idf", [P, 2 * T])
        iota_r = sb("iota_r", [P, N], bf16)
        idb = sb("idb", [P, P], bf16)
        dst_b = sb("dst_b", [P, E], bf16)
        Os = sb("Os", [P, T, N], bf16)
        onehot_dst = sb("onehot_dst", [P, T * N], bf16)
        Od = onehot_dst[:, :].rearrange("p (t n) -> p t n", t=T)
        OdT = onehot_dst[:, :].rearrange("p (a e) -> p a e", a=NH)
        OsR = sb("OsR", [P, RG, TG, N], fp32r)
        st6 = sb("st6", [P, NH, 6])
        mv1 = sb("mv1", [P, NH, 2])
        h1 = sb("h1", [P, NH, D])
        h1T = sb("h1T", [P, NH, KD, P])
        xb = sb("xb", [P, NH, D])
        ve = sb("ve", [P, NH])
        neghalf = sb("neghalf", [P, 2 * NH])
        CI = sb("CI", [P, NH, N], bf16)
        A = sb("A", [P, NH, N], fp32r)
        deg = sb("deg", [P, 2 * NH])
        scales = sb("scales", [P, 2 * NH])
        dinv, s1 = scales[:, 0:NH], scales[:, NH:2 * NH]
        hW_hi = sb("hW_hi", [P, NH, D], fp32r)
        hW_lo = sb("hW_lo", [P, NH, D], fp32r)
        x1 = sb("x1", [P, NH, D])
        xsum = sb("xsum", [P, NH])
        sq = sb("sq", [P, NH])
        h2, h2T = h1, h1T
        ve2 = sb("ve2", [P, NH])
        s2 = sb("s2", [P, NH])
        Hr = sb("Hr", [P, NH, C])
        Hp = [sb(f"Hp{i}", [P, NH, C], bf16) for i in range(3)]
        za = sb("za", [P, NG * P])
        hX = sb("hX", [P, NG * P], fp32r)
        hY = sb("hY", [P, NG * P], fp32r)
        ones = sb("ones", [96, P], bf16)
        b2r = sb("b2r", [64, P])
        b2p = sb("b2p", [96, P], bf16)
        y = sb("y", [P, T, 4])
        Wsb = w0_sb
        warmup = sb("warmup", [P, 512], bf16)
        WY = sb("WY", [P, T, S * F])
        late = dst_bc[:].bitcast(fp32)
        M = late[:, 0:RG * TG * S * F].rearrange("p (o b t n) -> p o b t n", o=RG, b=2, t=TG)
        tmp = late[:, RG * TG * S * F:RG * TG * (S + 3) * F].rearrange("p (o t n) -> p o t n", o=RG, t=TG)
        Mh = sb("Mh", [P, RG, 2, TG, 4 * F], fp32r)
        Ml = sb("Ml", [P, RG, 2, TG, 4 * F], fp32r)
        aggT = sb("aggT", [P, 2, N])
        wc_sb = sb("wc_sb", [P, B])
        ta, te, te2, os1T = (za[:, i * N:(i + 1) * N] for i in range(4))
        o_sb = x_sb
        warm = sb("warm", [P, 1])

        bank = [ctx.enter_context(nc.psum_tensor(f"bank{i}", [P, 512], fp32)) for i in range(8)]
        bT = bank[2][:, :].bitcast(bf16)

        (d_x, d_idx, d_dst, d_f, d_yr, d_w0, d_b0, d_w1, d_w2, d_b2, d_win, d_o1s, d_o1v, d_o2s, d_o2v, d_id,
         d_eye, d_out) = [sem("dma_" + n) for n in
                         "x idx dst f yr w0 b0 w1 w2 b2 win o1s o1v o2s o2v id eye out".split()]
        names = ("half warmup idf idb st mv1 ve h1 tp1 h1T hW "
                 "onehot onehot_p adj CI CT A degve scales hW_hi hW_lo L0 xb x1 "
                 "h2 neg_h2 tp2 h2T sq ve2 s2 H Hp0 Hr Hp1 Hp2 "
                 "z zabs zexp zln hT hhi hXlo hYlo w2hi w2lo ones b2r b2p W Wsb "
                 "y WYp WYd dstb OdT OsR "
                 "G part prod MA MB MhA MhB MlA MlB MlA_late MlB_late scat "
                 "scatA aggA aggT wc wcs o1 os1 ta te tl rl os1T fin os2 ov o")
        q = {n: sem("s_" + n) for n in names.split()}

        zb = (bank[2], bank[3], bank[7])
        gbank = (bank[0], bank[1], bank[7])
        fbank = [bank[i] for i in (3, 2, 0, 1, 3, 2, 3, 2, 3)]

        def weighted(g):
            own = [i for i in range(NG) if (i in POOL_FILTERS) == (g in POOL_FILTERS)]
            return q["WYp" if g in POOL_FILTERS else "WYd"], own.index(g) + 1

        def weight_filters(eng, wait_ge, g):
            t0, n = TG * g, tiles(g)
            w = Wsb[:, g % RW, 0:n * P].rearrange("p (t k f) -> p t k f", t=n, k=4)
            wy = WY[:, t0:t0 + n, :].rearrange("p t (k f) -> p t k f", k=S)
            yv = y[:, t0:t0 + n, 1:4].unsqueeze(3).broadcast_to((P, n, 3, F))
            y0 = y[:, t0:t0 + n, 0:1].unsqueeze(3).broadcast_to((P, n, 2, F))
            wait_ge(q["Wsb"], g + 1)
            wait_ge(q["y"], 1)
            eng.tensor_tensor(wy[:, :, 0:8:4, :], w[:, :, 0:2, :], y0, ALU.mult)
            eng.tensor_tensor(wy[:, :, 1:4, :], w[:, :, 2:3, :].broadcast_to((P, n, 3, F)), yv, ALU.mult)
            eng.tensor_tensor(wy[:, :, 5:8, :], w[:, :, 3:4, :].broadcast_to((P, n, 3, F)), yv,
                              ALU.mult).then_inc(weighted(g)[0], 1)

        block = ctx.enter_context(nc.Block())

        @block.sync
        def _(sp):
            sp.dma_start(idx_sb[:], idx).then_inc(d_idx, 16)
            sp.dma_start(w1_sb[:], w1).then_inc(d_w1, 16)
            sp.dma_start(x_sb[:, :, :], x.rearrange("(a p) d -> p a d", p=P)).then_inc(d_x, 16)
            sp.dma_start(w0_sb[:, :, :], w0.rearrange("(k p) n -> p k n", p=P)).then_inc(d_w0, 16)
            sp.dma_start(b0_sb[:], bias0.broadcast_to((P, D))).then_inc(d_b0, 16)
            sp.dma_start(win_sb[:], w_in).then_inc(d_win, 16)
            sp.dma_start(o1s_sb[:], w_o1s).then_inc(d_o1s, 16)
            sp.dma_start(dst_bc[:], dst_row.broadcast_to((P, E))).then_inc(d_dst, 16)
            sp.dma_start(o1vt_sb[:], w_o1vt).then_inc(d_o1v, 16)
            sp.dma_start(o2s_sb[:], w_o2s).then_inc(d_o2s, 16)
            sp.dma_start(o2v_sb[:], w_o2v).then_inc(d_o2v, 16)
            for a in range(NH):
                sp.wait_ge(q["ov"], a + 1)
                sp.dma_start(out[a * P:(a + 1) * P, B:], o_sb[:, a, B:]).then_inc(d_out, 16)
            sp.wait_ge(d_out, 16 * (NH + 1))

        @block.scalar
        def _(act):
            act.dma_start(f_sb[:], f_t).then_inc(d_f, 16)
            act.dma_start(id_iota[:], ident_iota).then_inc(d_id, 16)
            act.dma_start(w2_sb[:], w2).then_inc(d_w2, 16)
            act.dma_start(b2_sb[:], b2).then_inc(d_b2, 16)
            act.dma_start(yr_sb[:, :, :], yr).then_inc(d_yr, 16)
            act.dma_start(eye_sb[:, :, :], eye).then_inc(d_eye, 16)
            nc.scalar.preload_act_table_set("natural_log_exp_and_others")

            def absolute(c):
                lo, hi = 512 * c, min(512 * (c + 1), NG * P)
                act.wait_ge(q["z"], c + 1)
                nc.scalar.activation(za[:, lo:hi], zb[c][:, 0:hi - lo], ACT.Abs).then_inc(q["zabs"], 1)

            absolute(0)
            for a in range(NH):
                act.wait_ge(q["tp1"], a + 1)
                nc.scalar.activation(h1T[:, a, :, :], bank[(6, 1)[a]][:, :], ACT.Copy).then_inc(q["h1T"], 1)
            absolute(1)
            absolute(2)
            act.wait_ge(d_w2, 16)
            nc.scalar.activation(w2_hi[:], w2_sb[:], ACT.Copy).then_inc(q["w2hi"], 1)
            act.wait_ge(q["zabs"], 3)
            nc.scalar.activation(za[:], za[:], ACT.Exp, scale=-1.0).then_inc(q["zexp"], 1)
            act.wait_ge(q["zexp"], 1)
            act.wait_ge(q["half"], 1)
            nc.scalar.activation(za[:], za[:], ACT.Ln, bias=warm[:, 0:1], scale=0.5).then_inc(q["zln"], 1)
            act.wait_ge(q["hT"], 3)
            nc.scalar.activation(hX[0:64, :], za[0:64, :], ACT.Copy).then_inc(q["hhi"], 1)
            nc.scalar.activation(hY[64:128, :], za[64:128, :], ACT.Copy).then_inc(q["hhi"], 1)
            act.wait_ge(d_dst, 16)
            nc.scalar.activation(dst_b[:], dst_bc[:], ACT.Copy).then_inc(q["dstb"], 1)

            def scatter_onehots(g):
                t0, n = TG * g, tiles(g)
                act.wait_ge(q["onehot"], 2 * min(t0 + n, PT))
                if t0 + n > PT:
                    act.wait_ge(q["onehot_p"], 2 * (t0 + n - PT))
                if g >= RG:
                    act.wait_ge(q["scat"], g - RG + 1)
                nc.scalar.activation(OsR[:, g % RG, 0:n, :], Os[:, t0:t0 + n, :], ACT.Copy).then_inc(q["OsR"], 1)

            scatter_onehots(0)
            scatter_onehots(1)

            def filters_out(g):
                act.wait_ge(q["W"], g + 1)
                if g == 0:
                    act.wait_ge(q["hW"], NH)
                if g >= RW:
                    act.wait_ge(*weighted(g - RW))
                n = tiles(g)
                nc.scalar.activation(Wsb[:, g % RW, 0:n * P], fbank[g][:, 0:n * P], ACT.Copy).then_inc(q["Wsb"], 1)

            act.wait_ge(q["scales"], 1)
            for a in range(NH):
                act.wait_ge(q["hW"], a + 1)
                nc.scalar.activation(hW_hi[:, a, :], bank[a][:, :], ACT.Copy, scale=s1[:, a:a + 1]).then_inc(q["hW_hi"], 1)
            filters_out(0)
            act.wait_ge(q["x1"], 1)
            nc.scalar.activation(h2[:, 0, :], x1[:, 0, :], ACT.Identity, bias=xsum[:, 0:1],
                                 scale=-float(D)).then_inc(q["neg_h2"], 1)
            for a in range(NH):
                act.wait_ge(q[("neg_h2", "h2")[a]], 1)
                if a > 0:
                    act.wait_ge(q["sq"], a)
                nc.scalar.activation(za[:, 0:D], h2[:, a, :], ACT.Square, accum_out=sq[:, a:a + 1]).then_inc(q["sq"], 1)
            for g in range(1, 5):
                filters_out(g)
            scatter_onehots(2)
            filters_out(5)
            for g in range(NG):
                n = tiles(g)
                o = g % RG
                act.wait_ge(q["MB"], g + 1)
                if g >= RG:
                    act.wait_ge(q["scat"], g - RG + 1)
                nc.scalar.activation(Mh[:, o, 1, 0:n, :], M[:, o, 1, 0:n, :], ACT.Copy).then_inc(q["MhB"], 1)
                act.wait_ge(q["MA"], g + 1)
                nc.scalar.activation(Mh[:, o, 0, 0:n, :], M[:, o, 0, 0:n, :], ACT.Copy).then_inc(q["MhA"], 1)
                if g == 1:
                    act.wait_ge(q["wc"], 1)
                    nc.scalar.activation(wc_sb[:], bank[6][:, 0:B], ACT.Copy, scale=SF * SB).then_inc(q["wcs"], 1)
                if RG <= g + 1 < NG:
                    scatter_onehots(g + 1)
                if g in (0, 1, 3):
                    filters_out({0: 6, 1: 7, 3: 8}[g])
            act.wait_ge(q["scat"], NG)
            nc.scalar.activation(aggT[:, 1, :], bank[5][:, 0:N], ACT.Copy).then_inc(q["aggT"], 1)
            act.wait_ge(q["os1"], 1)
            nc.scalar.activation(ta[:], bank[2][:, 0:N], ACT.Abs, scale=SF).then_inc(q["ta"], 1)
            act.wait_ge(q["ta"], 1)
            nc.scalar.activation(te[:], ta[:], ACT.Exp, scale=-1.0).then_inc(q["te"], 1)
            act.wait_ge(q["te"], 1)
            nc.scalar.activation(ta[:], te[:], ACT.Ln, bias=warm[:, 0:1], scale=0.5).then_inc(q["tl"], 1)
            act.wait_ge(q["o"], NH)
            act.dma_start(out.rearrange("(a p) d -> p a d", p=P)[:, :, 0:B], o_sb[:, :, 0:B]).then_inc(d_out, 16)

        @block.gpsimd
        def _(pool):
            nc.gpsimd.memset(warm[:], 0.5).then_inc(q["half"], 1)
            nc.gpsimd.memset(neghalf[:], -0.5).then_inc(q["half"], 1)
            nc.gpsimd.memset(ones[:], 1.0).then_inc(q["ones"], 1)
            pool.wait_ge(q["idf"], 2)
            for t in range(PT, T):
                nc.gpsimd.tensor_scalar(Os[:, t, :], iota_r[:], idf[:, t:t + 1], None, ALU.is_equal).then_inc(q["onehot_p"], 1)
                nc.gpsimd.tensor_scalar(Od[:, t, :], iota_r[:], idf[:, T + t:T + t + 1], None,
                                        ALU.is_equal).then_inc(q["onehot_p"], 1)
            pool.wait_ge(d_b2, 16)
            nc.gpsimd.tensor_copy(b2p[:], b2_sb[:]).then_inc(q["b2p"], 1)
            pool.wait_ge(q["b2p"], 1)
            nc.gpsimd.tensor_tensor(b2r[:], b2_sb[0:64, :], b2p[0:64, :], ALU.subtract).then_inc(q["b2r"], 1)
            pool.wait_ge(q["b2r"], 1)
            nc.gpsimd.tensor_copy(b2p[0:64, :], b2r[:]).then_inc(q["b2p"], 1)
            pool.wait_ge(q["b2p"], 2)
            nc.gpsimd.tensor_tensor(b2p[0:32, :], b2r[0:32, :], b2p[0:32, :], ALU.subtract).then_inc(q["b2p"], 1)
            pool.wait_ge(q["b2p"], 3)
            pool.wait_ge(q["hhi"], 2)
            nc.gpsimd.tensor_tensor(hY[0:64, :], za[64:128, :], hY[64:128, :].bitcast(fp32),
                                    ALU.subtract).then_inc(q["hYlo"], 1)
            pool.wait_ge(q["hYlo"], 1)

            pool.wait_ge(q["degve"], 1)
            pool.wait_ge(q["half"], 2)
            nc.gpsimd.tensor_tensor(scales[:], deg[:], neghalf[:], ALU.pow).then_inc(q["scales"], 1)
            pool.wait_ge(d_b0, 16)
            pool.wait_ge(d_x, 16)
            nc.gpsimd.tensor_tensor(xb[:, :, :], x_sb[:, :, :], b0_sb[:].unsqueeze(1).broadcast_to((P, NH, D)),
                                    ALU.add).then_inc(q["xb"], 1)
            pool.wait_ge(d_yr, 16)
            nc.gpsimd.tensor_tensor(y[:, :, :], yr_sb[:, :, 0:4], yr_sb[:, :, 4:5].broadcast_to((P, T, 4)),
                                    ALU.mult).then_inc(q["y"], 1)
            weight_filters(nc.gpsimd, pool.wait_ge, 0)
            pool.wait_ge(q["sq"], NH)
            nc.gpsimd.tensor_scalar(ve2[:], sq[:], B / D, LN_EPS * D * D * B, ALU.mult, ALU.add).then_inc(q["ve2"], 1)
            pool.wait_ge(q["ve2"], 1)
            nc.gpsimd.tensor_tensor(s2[:], ve2[:], neghalf[:, 0:NH], ALU.pow).then_inc(q["s2"], 1)
            weight_filters(nc.gpsimd, pool.wait_ge, 1)
            weight_filters(nc.gpsimd, pool.wait_ge, 3)
            weight_filters(nc.gpsimd, pool.wait_ge, 4)
            for g in range(LATE):
                n = tiles(g)
                o = g % RG
                pool.wait_ge(q["MhB"], g + 1)
                if g >= RG:
                    pool.wait_ge(q["scat"], g - RG + 1)
                nc.gpsimd.tensor_tensor(Ml[:, o, 1, 0:n, :], M[:, o, 1, 0:n, :], Mh[:, o, 1, 0:n, :].bitcast(fp32),
                                        ALU.subtract).then_inc(q["MlB"], 1)
                if g < LATE - 1:
                    pool.wait_ge(q["MhA"], g + 1)
                    nc.gpsimd.tensor_tensor(Ml[:, o, 0, 0:n, :], M[:, o, 0, 0:n, :], Mh[:, o, 0, 0:n, :].bitcast(fp32),
                                            ALU.subtract).then_inc(q["MlA"], 1)

        @block.vector
        def _(dve):
            def onehots(t0, t1):
                for t in range(t0, t1):
                    nc.vector.tensor_scalar(Os[:, t, :], iota_r[:], idf[:, t:t + 1], None, ALU.is_equal).then_inc(q["onehot"], 1)
                    nc.vector.tensor_scalar(Od[:, t, :], iota_r[:], idf[:, T + t:T + t + 1], None,
                                            ALU.is_equal).then_inc(q["onehot"], 1)

            nc.vector.memset(warmup[:], 0.0).then_inc(q["warmup"], 1)
            dve.wait_ge(d_idx, 16)
            nc.vector.tensor_copy(iota_r[:], idx_sb[:, 2 * T:]).then_inc(q["idf"], 1)
            nc.vector.tensor_copy(idf[:], idx_sb[:, 0:2 * T]).then_inc(q["idf"], 1)
            dve.wait_ge(q["idf"], 2)
            onehots(0, 6)
            dve.wait_ge(d_x, 16)
            for a in range(NH):
                nc.vector.bn_stats(st6[:, a, :], x_sb[:, a, :]).then_inc(q["st"], 1)
                dve.wait_ge(q["st"], a + 1)
                nc.vector.bn_aggr(mv1[:, a, :], st6[:, a, :]).then_inc(q["mv1"], 1)
                dve.wait_ge(q["mv1"], a + 1)
                nc.vector.tensor_scalar(h1[:, a, :], x_sb[:, a, :], mv1[:, a, 0:1], 0.0, ALU.subtract,
                                        ALU.max).then_inc(q["h1"], 1)
            nc.vector.tensor_scalar(ve[:], mv1[:, :, 1], LN_EPS, None, ALU.add).then_inc(q["ve"], 1)
            onehots(6, 16)
            dve.wait_ge(d_id, 16)
            nc.vector.tensor_copy(idb[:], id_sb).then_inc(q["idb"], 1)
            dve.wait_ge(q["w2hi"], 1)
            nc.vector.tensor_tensor(w2_lo[:], w2_sb[:], w2_hi[:].bitcast(fp32), ALU.subtract).then_inc(q["w2lo"], 1)
            dve.wait_ge(d_o1s, 16)
            nc.vector.tensor_scalar(o1s_sb[F:2 * F, :], o1s_sb[F:2 * F, :], IS3, None, ALU.mult).then_inc(q["o1"], 1)
            dve.wait_ge(q["zln"], 1)
            for c in range(3):
                lo, hi = 512 * c, min(512 * (c + 1), NG * P)
                nc.vector.scalar_tensor_tensor(za[:, lo:hi], zb[c][:, 0:hi - lo], 0.0, za[:, lo:hi],
                                               ALU.max, ALU.add).then_inc(q["hT"], 1)
            onehots(16, PT)
            dve.wait_ge(q["adj"], 1)
            dve.wait_ge(d_eye, 16)
            for a in range(NH):
                nc.vector.scalar_tensor_tensor(CI[:, a, :], bank[4 + a][:, 0:N], 1.0, eye_sb[:, a, :], ALU.min,
                                               ALU.add).then_inc(q["CI"], 1)
            dve.wait_ge(q["CT"], 1)
            for a in range(NH):
                dve.wait_ge(q["CI"], a + 1)
                nc.vector.scalar_tensor_tensor(A[:, a, :], bT[:, a * N:(a + 1) * N], 0.0, CI[:, a, :], ALU.add,
                                               ALU.max, accum_out=deg[:, a:a + 1]).then_inc(q["A"], 1)
            dve.wait_ge(q["A"], NH)
            dve.wait_ge(q["ve"], 1)
            nc.vector.tensor_tensor(deg[:, NH:2 * NH], deg[:, 0:NH], ve[:], ALU.mult).then_inc(q["degve"], 1)

            def node_onehots(a, c):
                lo, hi = c * E // 2, (c + 1) * E // 2
                nc.vector.tensor_scalar(OdT[:, a, lo:hi], dst_b[:, lo:hi], iota_c[:, a:a + 1], None,
                                        ALU.is_equal).then_inc(q["OdT"], 1)

            dve.wait_ge(q["hhi"], 1)
            nc.vector.tensor_tensor(hX[64:128, :], za[0:64, :], hX[0:64, :].bitcast(fp32), ALU.subtract).then_inc(q["hXlo"], 1)
            dve.wait_ge(q["dstb"], 1)
            node_onehots(0, 0)
            for a in range(NH):
                dve.wait_ge(q["hW_hi"], a + 1)
                nc.vector.scalar_tensor_tensor(hW_lo[:, a, :], bank[a][:, :], s1[:, a:a + 1],
                                               hW_hi[:, a, :].bitcast(fp32), ALU.mult, ALU.subtract).then_inc(q["hW_lo"], 1)
            node_onehots(1, 0)
            dve.wait_ge(q["xb"], 1)
            for a in range(NH):
                dve.wait_ge(q["L0"], a + 1)
                nc.vector.scalar_tensor_tensor(x1[:, a, :], bank[4 + a][:, :], dinv[:, a:a + 1], xb[:, a, :], ALU.mult,
                                               ALU.add, accum_out=xsum[:, a:a + 1]).then_inc(q["x1"], 1)
            dve.wait_ge(q["x1"], 2)
            nc.vector.tensor_scalar(h2[:, 1, :], x1[:, 1, :], float(D), xsum[:, 1:2], ALU.mult,
                                    ALU.subtract).then_inc(q["h2"], 1)
            for a in range(NH):
                dve.wait_ge(q["tp2"], a + 1)
                nc.vector.tensor_scalar(h2T[:, a, :, :], bank[6 + a][:, :].rearrange("p (k n) -> p k n", k=KD),
                                        (-1.0, 1.0)[a], 0.0, ALU.mult, ALU.max).then_inc(q["h2T"], 1)
            node_onehots(0, 1)
            dve.wait_ge(q["s2"], 1)

            def high(a):
                dve.wait_ge(q["H"], a + 1)
                nc.vector.tensor_scalar(Hp[0][:, a, :], bank[6 + a][:, 0:C], s2[:, a:a + 1], None,
                                        ALU.mult).then_inc(q["Hp0"], 1)

            def rest(a):
                dve.wait_ge(q["Hp0"], a + 1)
                nc.vector.scalar_tensor_tensor(Hr[:, a, :], bank[6 + a][:, 0:C], s2[:, a:a + 1], Hp[0][:, a, :], ALU.mult,
                                               ALU.subtract).then_inc(q["Hr"], 1)

            def middle(a):
                dve.wait_ge(q["Hr"], a + 1)
                nc.vector.tensor_copy(Hp[1][:, a, :], Hr[:, a, :]).then_inc(q["Hp1"], 1)

            def low(a):
                dve.wait_ge(q["Hp1"], a + 1)
                nc.vector.tensor_tensor(Hp[2][:, a, :], Hr[:, a, :], Hp[1][:, a, :], ALU.subtract).then_inc(q["Hp2"], 1)

            high(0)
            rest(0)
            high(1)
            middle(0)
            rest(1)
            low(0)
            middle(1)
            low(1)
            weight_filters(nc.vector, dve.wait_ge, 2)
            for g in range(NG):
                t0, n, o = TG * g, tiles(g), g % RG
                G = gbank[o][:, 0:n * C].rearrange("p (t c f) -> p t c f", t=n, c=4)
                wy = WY[:, t0:t0 + n, :].rearrange("p t (k f) -> p t k f", k=S)
                mA, mB = (M[:, o, b, 0:n, :].rearrange("p t (k f) -> p t k f", k=4) for b in range(2))
                tc = tmp[:, o, 0:n, :].rearrange("p t (c f) -> p t c f", c=3)
                dve.wait_ge(q["G"], g + 1)
                dve.wait_ge(*weighted(g))
                if g >= RG:
                    dve.wait_ge(q["MlA"], g - RG + 1)
                sn = G[:, :, 0:1, :]
                nc.vector.tensor_tensor(mB[:, :, 0:4:2, :], sn.broadcast_to((P, n, 2, F)), wy[:, :, 2:4, :], ALU.mult)
                nc.vector.tensor_tensor(mB[:, :, 1:4:2, :], G[:, :, 2:4, :], wy[:, :, 4:5, :].broadcast_to((P, n, 2, F)),
                                        ALU.mult).then_inc(q["MB"], 1)
                nc.vector.tensor_tensor(tc, G[:, :, 1:4, :], wy[:, :, 5:8, :], ALU.mult).then_inc(q["part"], 1)
                nc.vector.tensor_tensor(mA[:, :, 0:4:2, :], sn.broadcast_to((P, n, 2, F)), wy[:, :, 0:2, :], ALU.mult)
                nc.vector.tensor_tensor(mA[:, :, 3, :], G[:, :, 1, :], wy[:, :, 4, :], ALU.mult).then_inc(q["prod"], 1)
                dve.wait_ge(q["part"], g + 1)
                nc.vector.tensor_reduce(mA[:, :, 1, :], tc.rearrange("p t c f -> p t f c"), mybir.AxisListType.X,
                                        ALU.add).then_inc(q["MA"], 1)
                if g == 0:
                    node_onehots(1, 1)
                elif g <= 4:
                    weight_filters(nc.vector, dve.wait_ge, g + 4)
            for g, b, rounded, left in ((LATE - 1, 0, "MhA", "MlA_late"), (LATE, 0, "MhA", "MlA_late"),
                                        (LATE, 1, "MhB", "MlB_late")):
                o, n = g % RG, tiles(g)
                dve.wait_ge(q[rounded], g + 1)
                nc.vector.tensor_tensor(Ml[:, o, b, 0:n, :], M[:, o, b, 0:n, :], Mh[:, o, b, 0:n, :].bitcast(fp32),
                                        ALU.subtract).then_inc(q[left], 1)
            dve.wait_ge(q["scatA"], 1)
            nc.vector.tensor_copy(aggT[:, 0, :], bank[4][:, 0:N]).then_inc(q["aggA"], 1)
            dve.wait_ge(q["ta"], 1)
            nc.vector.tensor_scalar(te2[:], bank[2][:, 0:N], SF, 0.0, ALU.mult, ALU.max).then_inc(q["rl"], 1)
            for a in range(NH):
                dve.wait_ge(q["fin"], a + 1)
                ov = o_sb[:, a, B:].rearrange("p (d c) -> p c d", c=3)
                xv = x1[:, a, B:].rearrange("p (d c) -> p c d", c=3)
                xz = bank[a][:, 0:2 * B].rearrange("p (c d) -> p c d", c=2)
                nc.vector.tensor_tensor(ov[:, 0:3:2, :], xz, xv[:, 0:3:2, :], ALU.add)
                nc.vector.tensor_tensor(ov[:, 1, :], bank[6 + a][:, 0:B], xv[:, 1, :], ALU.add).then_inc(q["ov"], 1)
                if a == 0:
                    dve.wait_ge(q["tl"], 1)
                    dve.wait_ge(q["rl"], 1)
                    nc.vector.tensor_tensor(os1T[:], te2[:], ta[:], ALU.add).then_inc(q["os1T"], 1)
            for a in range(NH):
                dve.wait_ge(q["os2"], a + 1)
                nc.vector.scalar_tensor_tensor(o_sb[:, a, 0:B], bank[2 + a][:, 0:B], SB, x1[:, a, 0:B], ALU.mult,
                                               ALU.add).then_inc(q["o"], 1)

        @block.tensor
        def _(pe):
            pe.wait_ge(q["warmup"], 1)
            for _ in range(WARM):
                nc.tensor.matmul(bank[0][:, :], warmup[:, 0:P], warmup[:], start=True, stop=True)

            def adjacency(ts):
                for t in ts:
                    if t < PT:
                        pe.wait_ge(q["onehot"], 2 * t + 2)
                    else:
                        pe.wait_ge(q["onehot_p"], 2 * (t - PT) + 2)
                    for a in range(NH):
                        last = nc.tensor.matmul(bank[4 + a][:, 0:N], Os[:, t, a * P:(a + 1) * P], Od[:, t, :],
                                                start=(t == 0), stop=(t == PT - 1))
                if t == PT - 1:
                    last.then_inc(q["adj"], 1)

            adjacency(range(0, 3))
            pe.wait_ge(d_f, 16)
            pe.wait_ge(d_w1, 16)

            def hidden(c):
                lo, hi = 512 * c, min(512 * (c + 1), NG * P)
                nc.tensor.matmul(zb[c][:, 0:hi - lo], w1_sb[:], f_sb[:, lo:hi], start=True, stop=True).then_inc(q["z"], 1)

            hidden(0)
            hidden(1)
            pe.wait_ge(d_id, 16)
            for a in range(NH):
                pe.wait_ge(q["h1"], a + 1)
                for k in range(KD):
                    last = nc.tensor.transpose(bank[(6, 1)[a]][:, k * P:(k + 1) * P], h1[:, a, k * P:(k + 1) * P], id_sb)
                last.then_inc(q["tp1"], 1)
                if a == 0:
                    adjacency(range(3, 5))
            hidden(2)
            pe.wait_ge(d_w0, 16)

            def first_layer(a, k0, k1):
                pe.wait_ge(q["h1T"], a + 1)
                for k in range(k0, k1):
                    last = nc.tensor.matmul(bank[a][:, :], h1T[:, a, k, :], w0_sb[:, k, :], start=(k == 0), stop=(k == KD - 1))
                if k1 == KD:
                    last.then_inc(q["hW"], 1)

            def filters(g):
                n = tiles(g)
                if g == 0:
                    pe.wait_ge(q["hXlo"], 1)
                    pe.wait_ge(q["hYlo"], 1)
                    pe.wait_ge(q["w2lo"], 1)
                    pe.wait_ge(q["b2p"], 3)
                    pe.wait_ge(q["ones"], 1)
                if g == 1:
                    pe.wait_ge(q["A"], NH)
                before = [i for i in range(g) if fbank[i] is fbank[g]]
                if before:
                    pe.wait_ge(q["Wsb"], before[-1] + 1)
                ps = fbank[g][:, 0:n * P]
                nc.tensor.matmul(ps, ones[:], b2p[:].unsqueeze(1).broadcast_to((96, n, P)), start=True, stop=False)
                for i, stack in enumerate((hX, hY)[0:n // 2]):
                    for part in (w2_hi, w2_lo):
                        last = nc.tensor.matmul(ps[:, 2 * P * i:2 * P * (i + 1)], stack[:, g * P:(g + 1) * P], part[:],
                                                start=False, stop=(2 * i + 2 == n and part is w2_lo))
                last.then_inc(q["W"], 1)

            first_layer(0, 0, KD)
            adjacency([5, *range(PT, T - 3), *range(6, 16), T - 3, T - 2, *range(16, 22), T - 1,
                       *range(22, PT)])
            first_layer(1, 0, 1)
            pe.wait_ge(q["idb"], 1)
            pe.wait_ge(q["CI"], NH)
            for a in range(NH):
                for b in range(NH):
                    last = nc.tensor.transpose(bT[:, a * N + b * P:a * N + (b + 1) * P], CI[:, b, a * P:(a + 1) * P], idb[:])
            last.then_inc(q["CT"], 1)
            first_layer(1, 1, KD)
            filters(0)
            for p, (part, ready) in enumerate(((hW_hi, "hW_hi"), (hW_lo, "hW_lo"))):
                for b in range(NH):
                    pe.wait_ge(q[ready], b + 1)
                    for a in range(NH):
                        last = nc.tensor.matmul(bank[4 + a][:, :], A[:, b, a * P:(a + 1) * P], part[:, b, :],
                                                start=(b == 0 and p == 0), stop=(b == NH - 1 and p == 1))
                        if b == NH - 1 and p == 1:
                            last.then_inc(q["L0"], 1)
            filters(1)
            filters(2)

            def transposes(a):
                pe.wait_ge(q[("neg_h2", "h2")[a]], 1)
                for k in range(4):
                    src = h2[:, a, 0:B] if k == 0 else h2[:, a, B:].rearrange("p (b c) -> p c b", c=3)[:, k - 1, :]
                    last = nc.tensor.transpose(bank[6 + a][:, k * P:(k + 1) * P], src, id_sb)
                last.then_inc(q["tp2"], 1)

            def node_channels(a):
                pe.wait_ge(q["h2T"], a + 1)
                for k in range(4):
                    w = win_sb[:, 0:F] if k == 0 else win_sb[:, F:2 * F]
                    last = nc.tensor.matmul(bank[6 + a][:, k * F:(k + 1) * F], h2T[:, a, k, :], w, start=True, stop=True)
                last.then_inc(q["H"], 1)

            transposes(0)
            transposes(1)
            filters(3)
            pe.wait_ge(d_win, 16)
            node_channels(0)
            node_channels(1)
            filters(4)
            filters(5)

            def gather(g):
                if g == 0:
                    pe.wait_ge(q["OdT"], NH)
                    pe.wait_ge(q["Hp2"], NH)
                if (TG * g + tiles(g)) * P > E // 2:
                    pe.wait_ge(q["OdT"], 2 * NH)
                if gbank[g % RG] in fbank:
                    pe.wait_ge(q["Wsb"], max(i for i in range(NG) if fbank[i] is gbank[g % RG]) + 1)
                if g >= RG:
                    pe.wait_ge(q["prod"], g - RG + 1)
                for j in range(tiles(g)):
                    t = TG * g + j
                    for a in range(NH):
                        for i in range(3):
                            last = nc.tensor.matmul(gbank[g % RG][:, j * C:(j + 1) * C], OdT[:, a, t * P:(t + 1) * P],
                                                    Hp[i][:, a, :], start=(a == 0 and i == 0), stop=(a == NH - 1 and i == 2))
                last.then_inc(q["G"], 1)

            def scatter(g):
                pe.wait_ge(q["OsR"], g + 1)
                for b in (1, 0) if g < LATE else (0, 1):
                    if g == LATE:
                        pe.wait_ge(q[("MlA_late", "MlB_late")[b]], 2 - b)
                    elif (g, b) == (LATE - 1, 0):
                        pe.wait_ge(q["MlA_late"], 1)
                    else:
                        pe.wait_ge(q[("MlA", "MlB")[b]], g + 1)
                    for j in range(tiles(g)):
                        t = TG * g + j
                        for part in (Mh, Ml):
                            last = nc.tensor.matmul(bank[4 + b][:, 0:N], part[:, g % RG, b, j, :], OsR[:, g % RG, j, :],
                                                    start=(t == 0 and part is Mh), stop=(t == T - 1 and part is Ml))
                    if g == LATE and b == 0:
                        last.then_inc(q["scatA"], 1)
                last.then_inc(q["scat"], 1)

            LAG = 2
            for g in range(NG + LAG):
                if g < NG:
                    gather(g)
                    if g in (0, 1, 3):
                        filters({0: 6, 1: 7, 3: 8}[g])
                if g == LAG:
                    pe.wait_ge(d_o1v, 16)
                    pe.wait_ge(d_o2v, 16)
                    nc.tensor.matmul(bank[6][:, 0:B], o1vt_sb[:], o2v_sb[:], start=True, stop=True).then_inc(q["wc"], 1)
                if g >= LAG:
                    scatter(g - LAG)
            pe.wait_ge(q["aggA"], 1)
            pe.wait_ge(q["o1"], 1)
            nc.tensor.matmul(bank[2][:, 0:N], o1s_sb[:], aggT[0:64, 0, :], start=True, stop=True).then_inc(q["os1"], 1)
            pe.wait_ge(q["aggT"], 1)
            pe.wait_ge(q["wcs"], 1)
            pe.wait_ge(d_o2s, 16)
            for a in range(NH):
                n = slice(a * P, (a + 1) * P)
                nc.tensor.matmul(bank[a][:, 0:B], aggT[64:128, 0, n], wc_sb[64:128, :], start=True, stop=True)
                nc.tensor.matmul(bank[a][:, B:2 * B], aggT[64:128, 1, n], wc_sb[64:128, :], start=True, stop=True)
                nc.tensor.matmul(bank[6 + a][:, 0:B], aggT[0:64, 1, n], wc_sb[0:64, :], start=True,
                                 stop=True).then_inc(q["fin"], 1)
            pe.wait_ge(q["os1T"], 1)
            for a in range(NH):
                n = slice(a * P, (a + 1) * P)
                nc.tensor.matmul(bank[2 + a][:, 0:B], os1T[:, n], o2s_sb[:], start=True, stop=True).then_inc(q["os2"], 1)


def kernel(x, src, dst, edge_attr_20, edge_attr_4, edge_weight, L0_gnn_weight, L0_gnn_bias, L1_gnn_w_in2f_s,
           L1_gnn_w_in2f_v, L1_gnn_W1, L1_gnn_b1, L1_gnn_W2, L1_gnn_b2, L1_gnn_w_f2o1_s, L1_gnn_w_f2o1_v,
           L1_gnn_w_f2o2_s, L1_gnn_w_f2o2_v):
    import ml_dtypes
    import numpy as np
    import concourse.bacc as bacc
    from concourse.bass_utils import run_bass_kernel_spmd

    g = {k: np.asarray(v) for k, v in locals().items() if isinstance(v, object) and hasattr(v, "shape")}
    P, TG = 128, 4
    E, R = g["edge_attr_20"].shape
    F = g["L1_gnn_W1"].shape[1]
    T = E // P
    NG = -(-T // TG)
    N = g["x"].shape[0]

    def edges_on_partitions(a):
        return np.ascontiguousarray(np.moveaxis(a.reshape(T, P, *a.shape[1:]), 0, 1))

    f = np.zeros((TG, R + 1, NG, P), np.float32)
    tiled = g["edge_attr_20"].reshape(T, P, R)
    for t in range(T):
        f[t % TG, :R, t // TG] = tiled[t].T
    f[:, R] = 1.0
    w1 = np.zeros((TG, R + 1, TG, F), np.float32)
    w2 = np.zeros((2, 2, F, 2, 4, F), np.float32)
    order = [0, 3, 2, 1]
    w2k = g["L1_gnn_W2"].reshape(F, F, 6).transpose(0, 2, 1)[:, order]
    b2k = g["L1_gnn_b2"].reshape(F, 6).T[order].reshape(-1)
    for j in range(TG):
        w1[j, :R, j] = g["L1_gnn_W1"]
        w1[j, R, j] = g["L1_gnn_b1"]
        w2[:, j % 2, :, j % 2] = w2k
    b2 = np.zeros((96, 4 * F), np.float32)
    b2[0::32] = b2k
    bf = ml_dtypes.bfloat16
    eye = np.zeros((P, N // P, N), bf)
    for a in range(N // P):
        eye[:, a, a * P:(a + 1) * P] = np.eye(P, dtype=bf)
    o1v_t = np.ascontiguousarray(g["L1_gnn_w_f2o1_v"].T)
    arrays = {
        "x": g["x"],
        "idx": np.concatenate([edges_on_partitions(g["src"]), edges_on_partitions(g["dst"]),
                               np.broadcast_to(np.arange(N, dtype=g["src"].dtype), (P, N))], 1),
        "dst_row": g["dst"].reshape(1, E),
        "f_t": f.reshape(TG * (R + 1), NG * P),
        "yr": np.concatenate([edges_on_partitions(g["edge_attr_4"]), edges_on_partitions(g["edge_weight"])[..., None]], 2),
        "w0": g["L0_gnn_weight"],
        "bias0": g["L0_gnn_bias"].reshape(1, -1),
        "w1": w1.reshape(TG * (R + 1), TG * F),
        "w2": w2.reshape(4 * F, 8 * F),
        "b2": b2,
        "w_in": np.concatenate([g["L1_gnn_w_in2f_s"], g["L1_gnn_w_in2f_v"]], 1),
        "w_o1s": g["L1_gnn_w_f2o1_s"],
        "w_o1vt": np.concatenate([o1v_t, o1v_t], 1),
        "w_o2s": g["L1_gnn_w_f2o2_s"],
        "w_o2v": g["L1_gnn_w_f2o2_v"],
        "eye": eye,
        "ident_iota": np.concatenate([np.eye(P, dtype=np.float32), np.arange(N, dtype=np.float32).reshape(N // P, P).T], 1),
    }
    arrays = {k: np.ascontiguousarray(v) for k, v in arrays.items()}
    nc = bacc.Bacc("TRN2", target_bir_lowering=False, num_devices=1)
    args = [nc.dram_tensor(k, v.shape, mybir.dt.from_np(v.dtype), kind="ExternalInput").ap() for k, v in arrays.items()]
    out = nc.dram_tensor("out", g["x"].shape, mybir.dt.float32, kind="ExternalOutput").ap()
    gnn_preln_kernel(nc, *args, out)
    r = run_bass_kernel_spmd(nc, [arrays], core_ids=[0])
    return r.results[0]["out"]
```
